# Optimizing a Trainium2 kernel written in Bass

```python
import numpy as np
import jax
import jax.numpy as jnp

def _softmax(x, axis=-1):
    return jax.nn.softmax(x, axis=axis)

def _gelu(x):
    return jax.nn.gelu(x, approximate=True)

def _silu(x):
    return jax.nn.silu(x)

def _sigmoid(x):
    return jax.nn.sigmoid(x)

def _layernorm(x, axis=-1, eps=1e-05):
    m = jnp.mean(x, axis=axis, keepdims=True)
    v = jnp.var(x, axis=axis, keepdims=True)
    return (x - m) / jnp.sqrt(v + eps)

def _scatter_add(tgt, idx, src, axis=0):
    return tgt.at[idx].add(src)

def _segment_sum(src, seg, n):
    return jax.ops.segment_sum(src, seg, n)
kernel_name = 'mk_flamingo_gated_d1_seqx_r8_813b7c'

def setup_inputs(seed: int=0):
    np.random.seed(seed)
    _w = jnp.asarray

    def _rec_inputs():
        import jax
        import jax.numpy as jnp
        _rk = jax.random.key(seed)
        x = -0.0002928 + 1 * jax.random.normal(jax.random.fold_in(_rk, 1), (128, 64, 128), jnp.float32)
        _lenS = 64 - jax.random.randint(jax.random.fold_in(_rk, 7), (128,), 0, max(1, 64 // 4) + 1, jnp.int32)
        _lenS2 = 64 - jax.random.randint(jax.random.fold_in(_rk, 8), (128,), 0, max(1, 64 // 4) + 1, jnp.int32)
        _ctx_1024P = jax.random.normal(jax.random.fold_in(_rk, 11), (128, 16, 128), jnp.float32)
        _ctx_1024c = jax.random.dirichlet(jax.random.fold_in(_rk, 511), 0.3 * jnp.ones((16,), jnp.float32), (128, 64))
        _ctx_1024t = jnp.einsum('bsk,bkd->bsd', _ctx_1024c, _ctx_1024P)
        _ctx_1024t = _ctx_1024t * jax.lax.rsqrt(jnp.mean(jnp.square(_ctx_1024t)) + 1e-12) * 0.953939
        ctx_1024 = -1.39393e-06 + 0.999914 * (_ctx_1024t + 0.3 * jax.random.normal(jax.random.fold_in(_rk, 611), (128, 64, 128), jnp.float32))
        _g = jax.random.normal(jax.random.fold_in(_rk, 9001), (2, 1), jnp.float32)
        _g = jnp.sign(_g) * jnp.maximum(jnp.abs(_g), 1.0) + (_g == 0) * 1.0
        g_xattn = _g[0]
        g_ffn = _g[1]
        return (x, ctx_1024, g_xattn, g_ffn)
    x, ctx_1024, g_xattn, g_ffn = _rec_inputs()

    def _L0_xattn_setup():
        import jax, jax.numpy as jnp
        import numpy as np
        D_MODEL = 128
        NUM_HEADS = 16
        D_HEAD = D_MODEL // NUM_HEADS
        WINDOW = 128

        def _to_heads(x):
            B, S, _ = x.shape
            return x.reshape(B, S, NUM_HEADS, D_HEAD).transpose(0, 2, 1, 3)
        key = jax.random.key(seed)
        ks = jax.random.split(key, 12)
        B, S, D = (2, 256, D_MODEL)
        scale = 1.0 / np.sqrt(D)
        inp = {'query': jax.random.normal(ks[0], (B, S, D), jnp.float32), 'key': jax.random.normal(ks[1], (B, S, D), jnp.float32), 'value': jax.random.normal(ks[2], (B, S, D), jnp.float32), 'Wq': jax.random.normal(ks[3], (D, D), jnp.float32) * scale, 'bq': jnp.zeros((D,), jnp.float32), 'Wk': jax.random.normal(ks[4], (D, D), jnp.float32) * scale, 'bk': jnp.zeros((D,), jnp.float32), 'Wv': jax.random.normal(ks[5], (D, D), jnp.float32) * scale, 'bv': jnp.zeros((D,), jnp.float32), 'Wo': jax.random.normal(ks[6], (D, D), jnp.float32) * scale, 'bo': jnp.zeros((D,), jnp.float32)}
        return inp
    _L0_xattn_all = _L0_xattn_setup()
    _L0_xattn_in = {k: v for k, v in _L0_xattn_all.items() if k in ('Wq', 'bq', 'Wk', 'bk', 'Wv', 'bv', 'Wo', 'bo')}
    del _L0_xattn_all

    def _L0_ffn_setup():
        import jax, jax.numpy as jnp
        import numpy as np
        B, L, H = (8, 256, 128)
        E, K, R = (8, 2, 64)

        def _gates(cls_tok, Wr):
            logits = cls_tok @ Wr.T
            top_vals, top_idx = jax.lax.top_k(logits, K)
            neg_inf = jnp.full_like(logits, -jnp.inf)
            rows = jnp.arange(logits.shape[0])[:, None]
            masked = neg_inf.at[rows, top_idx].set(top_vals)
            return jax.nn.softmax(masked, axis=-1)
        key = jax.random.key(seed)
        k1, k2, k3, k4 = jax.random.split(key, 4)
        x = jax.random.normal(k1, (B, L, H), dtype=jnp.float32)
        Wr = jax.random.normal(k2, (E, H), dtype=jnp.float32) * (1.0 / np.sqrt(H))
        A = jax.random.normal(k3, (E, R, H), dtype=jnp.float32) * (1.0 / np.sqrt(H))
        Bw = jax.random.normal(k4, (E, H, R), dtype=jnp.float32) * (1.0 / np.sqrt(R))
        return {'x': x, 'Wr': Wr, 'A': A, 'Bw': Bw}
    _L0_ffn_all = _L0_ffn_setup()
    _L0_ffn_in = {k: v for k, v in _L0_ffn_all.items() if k in ('Wr', 'A', 'Bw')}
    del _L0_ffn_all
    return {'x': x, 'ctx_1024': ctx_1024, 'g_xattn': g_xattn, 'g_ffn': g_ffn, 'L0_xattn_Wq': _L0_xattn_in['Wq'], 'L0_xattn_bq': _L0_xattn_in['bq'], 'L0_xattn_Wk': _L0_xattn_in['Wk'], 'L0_xattn_bk': _L0_xattn_in['bk'], 'L0_xattn_Wv': _L0_xattn_in['Wv'], 'L0_xattn_bv': _L0_xattn_in['bv'], 'L0_xattn_Wo': _L0_xattn_in['Wo'], 'L0_xattn_bo': _L0_xattn_in['bo'], 'L0_ffn_Wr': _L0_ffn_in['Wr'], 'L0_ffn_A': _L0_ffn_in['A'], 'L0_ffn_Bw': _L0_ffn_in['Bw']}

def reference(x, ctx_1024, g_xattn, g_ffn, L0_xattn_Wq, L0_xattn_bq, L0_xattn_Wk, L0_xattn_bk, L0_xattn_Wv, L0_xattn_bv, L0_xattn_Wo, L0_xattn_bo, L0_ffn_Wr, L0_ffn_A, L0_ffn_Bw):
    import jax
    import jax.numpy as jnp

    def _L0_xattn_ref(query, key, value, Wq, bq, Wk, bk, Wv, bv, Wo, bo):
        import jax, jax.numpy as jnp
        import numpy as np
        D_MODEL = 128
        NUM_HEADS = 16
        D_HEAD = D_MODEL // NUM_HEADS
        WINDOW = 128

        def _to_heads(x):
            B, S, _ = x.shape
            return x.reshape(B, S, NUM_HEADS, D_HEAD).transpose(0, 2, 1, 3)
        B, S, D = query.shape
        q = _to_heads(query @ Wq + bq)
        k = _to_heads(key @ Wk + bk)
        v = _to_heads(value @ Wv + bv)
        scores = jnp.einsum('bhqd,bhkd->bhqk', q, k) / jnp.sqrt(jnp.float32(D_HEAD))
        i = jnp.arange(S)[:, None]
        j = jnp.arange(S)[None, :]
        local_mask = jnp.abs(i - j) <= WINDOW // 2
        scores = jnp.where(local_mask[None, None], scores, -jnp.inf)
        attn = jax.nn.softmax(scores, axis=-1)
        ctx = jnp.einsum('bhqk,bhkd->bhqd', attn, v)
        ctx = ctx.transpose(0, 2, 1, 3).reshape(B, S, D)
        return ctx @ Wo + bo

    def _L0_ffn_ref(x, Wr, A, Bw):
        import jax, jax.numpy as jnp
        import numpy as np
        B, L, H = (8, 256, 128)
        E, K, R = (8, 2, 64)

        def _gates(cls_tok, Wr):
            logits = cls_tok @ Wr.T
            top_vals, top_idx = jax.lax.top_k(logits, K)
            neg_inf = jnp.full_like(logits, -jnp.inf)
            rows = jnp.arange(logits.shape[0])[:, None]
            masked = neg_inf.at[rows, top_idx].set(top_vals)
            return jax.nn.softmax(masked, axis=-1)
        gates = _gates(x[:, 0, :], Wr)
        mid = jnp.einsum('blh,erh->belr', x, A)
        expert_out = jnp.einsum('belr,ehr->belh', mid, Bw)
        weighted = jnp.einsum('be,belh->blh', gates, expert_out)
        return x + weighted
    x = x + jnp.tanh(g_xattn[0]) * _L0_xattn_ref(_layernorm(x, axis=-1), ctx_1024, ctx_1024, L0_xattn_Wq, L0_xattn_bq, L0_xattn_Wk, L0_xattn_bk, L0_xattn_Wv, L0_xattn_bv, L0_xattn_Wo, L0_xattn_bo)
    x = x + jnp.tanh(g_ffn[0]) * _L0_ffn_ref(_layernorm(x, axis=-1), L0_ffn_Wr, L0_ffn_A, L0_ffn_Bw)
    return x

_drawn_inputs = setup_inputs


def setup_inputs(seed=0):
    import zlib

    import numpy as np

    out = dict(_drawn_inputs(seed))
    spreads = {'L0_xattn_bq': (0.0, 0.1),
     'L0_xattn_bk': (0.0, 0.1),
     'L0_xattn_bv': (0.0, 0.1),
     'L0_xattn_bo': (0.0, 0.1)}
    factors = {}
    for name, (base, spread) in spreads.items():
        noise = np.random.default_rng([zlib.crc32(name.encode()), seed]).standard_normal(out[name].shape)
        drawn = base * np.exp(spread * noise) if base else spread * noise
        out[name] = jnp.asarray(drawn.astype(out[name].dtype))
    for name, factor in factors.items():
        out[name] = (out[name] * factor).astype(out[name].dtype)
    return out
```

```python
from contextlib import ExitStack

import concourse.bass as bass
from concourse import mybir

P = 128
BATCHES, SEQ, D = 128, 64, 128
HEADS, DH = 16, 8
PAIRS = HEADS // 2
EXPERTS, RANK = 8, 64
CB = 8
CHUNKS = BATCHES // CB
TOK = CB * SEQ
TILES = TOK // P
Q_PART = (0, 1, 2, 0, 1, 0)
K_PART = (0, 0, 0, 1, 1, 2)
TERMS = len(Q_PART)
ROWS = TERMS * 2 * DH
SHIFT = 4
VW = 32
HC = D // 16
EPS = 1e-5

ALU = mybir.AluOpType
ACT = mybir.ActivationFunctionType
BF16 = mybir.dt.bfloat16
F32 = mybir.dt.float32
U32 = mybir.dt.uint32
AX_X = mybir.AxisListType.X

FIRST, LAST = -3, CHUNKS + 1
LOOP_FIRST = 3
LOOP_TURNS = (CHUNKS - 3 - LOOP_FIRST) // 2
LOOP_END = LOOP_FIRST + 2 * LOOP_TURNS


def block_attention_experts(nc, x, ctx_in, g_xattn, g_ffn, Wq, bq, Wk, bk, Wv, bv, Wo, bo, Wr, A, Bw, out):
    x_v = x.rearrange("(c t b) s d -> c (b s) t d", t=TILES, b=2)
    c_v = ctx_in.rearrange("(c t b) s d -> c (b s) t d", t=TILES, b=2)
    o_v = out.rearrange("(c t b) s d -> c (b s) t d", t=TILES, b=2)

    stack = ExitStack()
    with stack:
        def sb(name, shape, dt=F32):
            return stack.enter_context(nc.sbuf_tensor(name, shape, dt))

        def pb(name, shape, dt=F32):
            return stack.enter_context(nc.psum_tensor(name, shape, dt))

        def sem(name):
            return stack.enter_context(nc.semaphore(name))

        def two(make, name, shape, dt=F32):
            return [make(f"{name}{n}", shape, dt) for n in range(2)]

        ident = sb("ident", [P, P])
        identb = sb("identb", [P, P], BF16)
        ones_f = sb("ones_f", [1, P])
        one_f = sb("one_f", [P, 1])
        minus_half = sb("minus_half", [P, TILES])
        ones_b = sb("ones_b", [PAIRS, TOK], BF16)
        col_of = sb("col_of", [CB, EXPERTS])
        h16_mask = sb("h16_mask", [P, 16])
        wq, wk, wv, wo, wo_g = (sb(n, [P, D]) for n in ("wq", "wk", "wv", "wo", "wo_g"))
        wq_p, wk_p = sb("wq_p", [P, D]), sb("wk_p", [P, D])
        b_row = sb("b_row", [1, 2, D])
        b_rowp = sb("b_rowp", [1, 2, D])
        bias = sb("bias", [P, 2])
        bv_col = sb("bv_col", [P, 1])
        bo_row = sb("bo_row", [1, D])
        bv_rep = sb("bv_rep", [P, P])
        g_row = sb("g_row", [1, 2])
        tg = sb("tg", [P, 2])
        c_rep = sb("c_rep", [P, D])
        wr_in = sb("wr_in", [EXPERTS, D])
        wrT = sb("wrT", [D, EXPERTS])
        a_in = sb("a_in", [P, EXPERTS // 2, D])
        bw_in = sb("bw_in", [D, EXPERTS // 2, P])
        bwT = sb("bwT", [P, EXPERTS // 2, D])
        mix_h = sb("mix_h", [P, EXPERTS, D])
        mix = sb("mix", [P, HC, D])

        xt = two(sb, "xt", [P, TILES, D])
        ct = two(sb, "ct", [P, TILES, D])
        stats1 = sb("stats1", [P, TILES, 6])
        work1 = sb("work1", [P, 8, TILES])
        stats2 = sb("stats2", [P, TILES, 6])
        work2 = sb("work2", [P, 10, TILES])
        xn = sb("xn", [P, TILES, D])
        xnT = sb("xnT", [D, TOK])
        cT = sb("cT", [D, TOK])
        qp = sb("qp", [P, 3, TOK], BF16)
        kp = sb("kp", [P, 3, TOK], BF16)
        q_rest = sb("q_rest", [P, TOK])
        k_rest = sb("k_rest", [P, TOK])
        qa = two(sb, "qa", [P, PAIRS, TOK], BF16)
        kb = two(sb, "kb", [P, PAIRS, CB, 2, SEQ], BF16)
        vb = two(sb, "vb", [P, CB, PAIRS, VW])
        nmax = sb("nmax", [P, 2, PAIRS, TILES])
        shift = sb("shift", [P, 2, 2 * PAIRS * TILES], BF16)
        shiftT = sb("shiftT", [P, P], BF16)
        prob = sb("prob", [P, PAIRS, TOK])
        oaug = sb("oaug", [P, 2, TOK])
        rden = sb("rden", [P, 2, 32])
        o_tok = sb("o_tok", [P, TILES, D])
        oT = sb("oT", [D, TOK])
        xr = two(sb, "xr", [P, TILES, D])
        x1 = two(sb, "x1", [P, TILES, D])
        xn2 = sb("xn2", [P, TILES, D])
        x2T = sb("x2T", [D, TOK])
        logit = sb("logit", [CB, EXPERTS])
        top = sb("top", [CB, EXPERTS])
        top_i = sb("top_i", [CB, EXPERTS], U32)
        top_f = sb("top_f", [CB, EXPERTS])
        gw = sb("gw", [CB, 6])
        gate_a = sb("gate_a", [CB, EXPERTS])
        gate_b = sb("gate_b", [CB, EXPERTS])
        gates = sb("gates", [CB, 16, EXPERTS])
        gmix = sb("gmix", [P, CB, 16])
        wmix = sb("wmix", [D, CB, D])

        ps_s = two(pb, "ps_s", [P, TOK])
        ps_t = two(pb, "ps_t", [P, TOK])
        ps_o = pb("ps_o", [P, TOK])
        bank = [pb(f"bank{n}", [P, TOK]) for n in range(3)]

        w_in = sem("w_in")
        pool_waited, dve_waited = sem("pool_waited"), sem("dve_waited")
        mix_in = sem("mix_in")
        kb_ones = sem("kb_ones")
        consts = sem("consts")
        consts2 = sem("consts2")
        kb_cleared, vb_cleared, vb_ones = sem("kb_cleared"), sem("vb_cleared"), sem("vb_ones")
        set_pe = sem("set_pe")
        set_dve = sem("set_dve")
        set_act = sem("set_act")
        x_in = [sem(f"x_in{n}") for n in range(2)]
        c_in = [sem(f"c_in{n}") for n in range(2)]
        xr_in = [sem(f"xr_in{n}") for n in range(2)]
        qa_in = [sem(f"qa_in{n}") for n in range(2)]
        kb_in = [sem(f"kb_in{n}") for n in range(2)]
        shift_in = [sem(f"shift_in{n}") for n in range(2)]
        out_done = [sem(f"out_done{n}") for n in range(2)]
        ln1_steps = sem("ln1_steps")
        ln2_steps = sem("ln2_steps")
        rstd1_ready, rstd2_ready = sem("rstd1_ready"), sem("rstd2_ready")
        xn_ready = sem("xn_ready")
        xnT_filled, xnT_taken = sem("xnT_filled"), sem("xnT_taken")
        cT_filled, cT_taken = sem("cT_filled"), sem("cT_taken")
        q_filled, q_high, q_taken, q_mid, q_parts = (sem(n) for n in ("q_filled", "q_high", "q_taken", "q_mid", "q_parts"))
        k_filled, k_high, k_taken, k_mid, k_parts = (sem(n) for n in ("k_filled", "k_high", "k_taken", "k_mid", "k_parts"))
        v_filled, v_low, v_high = sem("v_filled"), sem("v_low"), sem("v_high")
        s_filled, s_max = sem("s_filled"), sem("s_max")
        shift_hi, shift_ready = sem("shift_hi"), sem("shift_ready")
        shiftT_filled, shiftT_taken = sem("shiftT_filled"), sem("shiftT_taken")
        t_filled, t_exp = sem("t_filled"), sem("t_exp")
        o_filled, o_taken = sem("o_filled"), sem("o_taken")
        otr_filled, rden_ready, o_normed = sem("otr_filled"), sem("rden_ready"), sem("o_normed")
        oT_filled, oT_taken = sem("oT_filled"), sem("oT_taken")
        xr_ready = sem("xr_ready")
        y_filled, x1_ready = sem("y_filled"), sem("x1_ready")
        xn2_ready, x1_scaled = sem("xn2_ready"), sem("x1_scaled")
        x2T_filled, x2T_taken = sem("x2T_filled"), sem("x2T_taken")
        logit_filled, gate_steps, gate_diff, gate_exp, gates_ready = (
            sem(n) for n in ("logit_filled", "gate_steps", "gate_diff", "gate_exp", "gates_ready"))
        grep_filled, gmix_ready = sem("grep_filled"), sem("gmix_ready")
        wmix_filled, wmix_taken = sem("wmix_filled"), sem("wmix_taken")
        y2_filled, out_ready = sem("y2_filled"), sem("out_ready")

        block = stack.enter_context(nc.Block())

        def steps(eng, step):
            for i in range(FIRST, LOOP_FIRST):
                step(0, i)
            with eng.Fori(0, LOOP_TURNS) as turn:
                step(turn, LOOP_FIRST)
                step(turn, LOOP_FIRST + 1)
            for i in range(LOOP_END, LAST + 1):
                step(0, i)

        def has(c):
            return 0 <= c < CHUNKS

        def wait_chunk(eng, s, per, turn, c, n):
            if per * c + n > 0 and c >= 0:
                eng.wait_ge(s, 2 * per * turn + (per * c + n))

        def wait_half(eng, pair_of_sems, per, turn, c):
            if c >= 0:
                eng.wait_ge(pair_of_sems[c % 2], per * turn + per * (c // 2 + 1))

        @block.sync
        def _(sp):
            for dst, src in ((wq[:], Wq), (wk[:], Wk), (wv[:], Wv), (wo[:], Wo),
                             (b_row[:, 0, :], bq.rearrange("(o n) -> o n", o=1)),
                             (b_row[:, 1, :], bk.rearrange("(o n) -> o n", o=1)),
                             (bv_col[:], bv.rearrange("(p o) -> p o", o=1)),
                             (bo_row[:], bo.rearrange("(o n) -> o n", o=1)),
                             (g_row[:, 0:1], g_xattn.rearrange("(o n) -> o n", o=1)),
                             (g_row[:, 1:2], g_ffn.rearrange("(o n) -> o n", o=1)),
                             (wr_in[:], Wr),
                             (a_in[:], A.rearrange("(e4 e2) r d -> (e2 r) e4 d", e2=2)),
                             (bw_in[:].rearrange("h e4 (e2 r) -> h (e4 e2) r", e2=2), Bw.rearrange("e h r -> h e r"))):
                sp.dma_start(dst, src).then_inc(w_in, 16)

            def setup_rest():
                sp.wait_ge(consts2, 1)
                sp.wait_ge(kb_cleared, 2)
                for n in range(2):
                    for part in range(2):
                        for h2 in range(2):
                            row = ROWS + 2 * part + h2
                            sp.dma_start(kb[n][row:row + 1, :, :, h2, :], ones_b[:, :]).then_inc(kb_ones, 16)
                sp.wait_ge(set_dve, 9)
                for hc in range(HC):
                    sp.dma_start(mix[:, hc, :], mix_h[16 * hc:16 * hc + 16, :, :]).then_inc(mix_in, 16)

            def step(turn, i):
                l, b, q, f = i + 3, i + 1, i - 1, i - 2
                if i == -2:
                    setup_rest()
                if has(b):
                    pass
                if has(l):
                    wait_chunk(sp, xn_ready, TILES, turn, l - 2, TILES)
                    sp.dma_start(xt[l % 2][:], x_v[bass.ds(2 * turn + l, 1)].rearrange("o p t d -> p (o t) d")).then_inc(x_in[l % 2], 16)
                    wait_chunk(sp, cT_filled, 1, turn, l - 2, 1)
                    sp.dma_start(ct[l % 2][:], c_v[bass.ds(2 * turn + l, 1)].rearrange("o p t d -> p (o t) d")).then_inc(c_in[l % 2], 16)
                if has(i):
                    wait_chunk(sp, x1_ready, 1, turn, i - 2, 1)
                    sp.dma_start(xr[i % 2][:], x_v[bass.ds(2 * turn + i, 1)].rearrange("o p t d -> p (o t) d")).then_inc(xr_in[i % 2], 16)
                if has(b):
                    n = b % 2
                    if b < 2:
                        sp.wait_ge(kb_ones, 128)
                    wait_chunk(sp, t_filled, PAIRS, turn, b - 2, PAIRS)
                    wait_chunk(sp, q_parts, 1, turn, b, 1)
                    for t in range(TERMS):
                        sp.dma_start(qa[n][16 * t:16 * t + 16, :, :], qp[:, Q_PART[t], :]).then_inc(qa_in[n], 16)
                    wait_chunk(sp, k_parts, 1, turn, b, 1)
                    for t in range(TERMS):
                        for h2 in range(2):
                            r = 16 * t + 8 * h2
                            sp.dma_start(kb[n][r:r + DH, :, :, h2, :], kp[64 * h2:64 * h2 + 64, K_PART[t], :]).then_inc(kb_in[n], 16)
                if has(i):
                    wait_chunk(sp, shiftT_taken, 1, turn, i, 1)
                    sp.dma_start(qa[i % 2][ROWS:ROWS + SHIFT, :, :].rearrange("r a n -> r (a n)"), shiftT[:, :]).then_inc(shift_in[i % 2], 16)
                if has(f):
                    wait_chunk(sp, out_ready, 1, turn, f, 1)
                    sp.dma_start(o_v[bass.ds(2 * turn + f, 1)].rearrange("o p t d -> p (o t) d"), x1[f % 2][:]).then_inc(out_done[f % 2], 16)

            steps(sp, step)
            for n in range(2):
                sp.wait_ge(out_done[n], 16 * CHUNKS // 2)

        @block.gpsimd
        def _(pool):
            pool.memset(ident[:], 0.0).then_inc(consts, 1)
            pool.memset(identb[:], 0.0).then_inc(consts, 1)
            pool.memset(h16_mask[:], 1.0).then_inc(consts, 1)
            pool.memset(ones_b[:], 1.0).then_inc(consts2, 1)
            pool.memset(minus_half[:], -0.5).then_inc(consts, 1)
            pool.memset(ones_f[:], 1.0).then_inc(consts, 1)
            pool.memset(one_f[:], 1.0).then_inc(consts, 1)
            pool.iota(top_i[:], [[1, EXPERTS]], base=0, channel_multiplier=0).then_inc(consts, 1)
            pool.wait_ge(consts, 7)
            pool.tensor_copy(col_of[:], top_i[:]).then_inc(consts, 1)
            for m in (ident, identb):
                pool.affine_select(out=m[:], in_=m[:], compare_op=ALU.not_equal, fill=1.0,
                                   base=0, pattern=[[-1, P]], channel_multiplier=1).then_inc(consts, 1)
            pool.affine_select(out=h16_mask[:], in_=h16_mask[:], compare_op=ALU.is_ge, fill=0.0,
                               base=0, pattern=[[-8, 16]], channel_multiplier=1).then_inc(consts, 1)
            pool.wait_ge(consts, 11)
            pool.affine_select(out=h16_mask[:], in_=h16_mask[:], compare_op=ALU.is_ge, fill=0.0,
                               base=7, pattern=[[8, 16]], channel_multiplier=-1).then_inc(consts, 1)
            for n in range(2):
                pool.memset(kb[n][:].rearrange("p a b g k -> p (a b g k)").bitcast(F32), 0.0).then_inc(kb_cleared, 1)

            pool.wait_ge(consts, 12)

            def rstd(steps_sem, work, done, n, turn, c):
                wait_chunk(pool, steps_sem, 8, turn, c, 8)
                pool.tensor_tensor(work[:, 6, :], work[:, 5, :], minus_half[:], ALU.pow).then_inc(done, 1)
                wait_chunk(pool, done, n, turn, c, 1)
                pool.tensor_tensor(work[:, 7, :], work[:, 0, :], work[:, 6, :], ALU.mult).then_inc(done, 1)

            def low_part(ready, p, rest, done, turn, b):
                wait_chunk(pool, ready, 1, turn, b, 1)
                pool.tensor_tensor(p[:, 2, :], rest[:], p[:, 1, :], ALU.subtract).then_inc(done, 1)

            def step(turn, i):
                a, b, q, f = i + 2, i + 1, i - 1, i - 2
                if has(b):
                    low_part(q_mid, qp, q_rest, q_parts, turn, b)
                    low_part(k_mid, kp, k_rest, k_parts, turn, b)
                if has(f):
                    for t in range(TILES):
                        if t == 0:
                            wait_chunk(pool, xn2_ready, TILES, turn, f, TILES)
                            pool.sem_inc(pool_waited, 1)
                        pool.tensor_scalar(x1[f % 2][:, t, :], x1[f % 2][:, t, :], work2[:, 8, t:t + 1], work2[:, 9, t:t + 1],
                                           ALU.mult, ALU.add).then_inc(x1_scaled, 1)
                if has(a):
                    rstd(ln1_steps, work1, rstd1_ready, 2, turn, a)
                    wait_chunk(pool, rstd1_ready, 2, turn, a, 2)
                    wait_chunk(pool, xnT_filled, 1, turn, a - 1, 1)
                    wait_half(pool, x_in, 16, turn, a)
                    pool.sem_inc(pool_waited, 1)
                    for t in range(TILES):
                        pool.tensor_scalar(xn[:, t, :], xt[a % 2][:, t, :], work1[:, 6, t:t + 1], work1[:, 7, t:t + 1],
                                           ALU.mult, ALU.add).then_inc(xn_ready, 1)
                if has(q):
                    if q == 0:
                        pool.wait_ge(set_dve, 11)
                    wait_half(pool, xr_in, 16, turn, q)
                    pool.tensor_tensor(xr[q % 2][:], xr[q % 2][:], c_rep[:, None, :].to_broadcast([P, TILES, D]),
                                       ALU.add).then_inc(xr_ready, 1)
                    rstd(ln2_steps, work2, rstd2_ready, 4, turn, q)
                    wait_chunk(pool, rstd2_ready, 4, turn, q, 2)
                    pool.sem_inc(pool_waited, 1)
                    pool.tensor_scalar(work2[:, 8, :], work2[:, 6, :], tg[:, 1:2], one_f[:, 0:1], ALU.mult, ALU.add).then_inc(rstd2_ready, 1)
                    wait_chunk(pool, rstd2_ready, 4, turn, q, 3)
                    pool.sem_inc(pool_waited, 1)
                    pool.tensor_scalar(work2[:, 9, :], work2[:, 7, :], tg[:, 1:2], None, ALU.mult).then_inc(rstd2_ready, 1)
                    wait_chunk(pool, rstd2_ready, 4, turn, q, 4)
                    wait_chunk(pool, x2T_filled, 1, turn, q - 1, 1)
                    pool.sem_inc(pool_waited, 1)
                    for t in range(TILES):
                        pool.tensor_scalar(xn2[:, t, :], x1[q % 2][:, t, :], work2[:, 6, t:t + 1], work2[:, 7, t:t + 1],
                                           ALU.mult, ALU.add).then_inc(xn2_ready, 1)

            steps(pool, step)

        @block.scalar
        def _(act):
            act.wait_ge(vb_ones, 4)
            act.wait_ge(set_pe, 1)
            nc.scalar.activation(tg[:], bank[0][:, 0:2], ACT.Tanh).then_inc(set_act, 1)

            def copy(dst, src, filled, per, turn, c, n, done):
                wait_chunk(act, filled, per, turn, c, n)
                nc.scalar.activation(dst, src, ACT.Copy).then_inc(done, 1)

            def high_part(p, src, col, filled, high, landed, per, turn, b):
                wait_half(act, landed, per, turn, b - 1)
                wait_chunk(act, filled, 1, turn, b, 1)
                nc.scalar.activation(p[:, 0, :], src[:], ACT.Identity, bias=bias[:, col:col + 1]).then_inc(high, 1)

            def exp(turn, q, pair):
                wait_chunk(act, t_filled, PAIRS, turn, q, pair + 1)
                wait_chunk(act, o_filled, 2, turn, q - 1, pair // 4 + 1)
                nc.scalar.activation(prob[:, pair, :], ps_t[pair % 2][:], ACT.Exp, scale=DH ** -0.5).then_inc(t_exp, 1)

            def step(turn, i):
                b, q, f = i + 1, i - 1, i - 2
                if has(b):
                    wait_chunk(act, k_filled, 1, turn, b - 1, 1)
                    wait_chunk(act, v_filled, 1, turn, b - 1, 1)
                    copy(xnT[:], bank[0][:], xnT_filled, 1, turn, b, 1, xnT_taken)
                    copy(cT[:], bank[1][:], cT_filled, 1, turn, b, 1, cT_taken)
                if has(q):
                    exp(turn, q, 0)
                    exp(turn, q, 1)
                if has(b):
                    high_part(qp, bank[1], 0, q_filled, q_high, qa_in, 16 * TERMS, turn, b)
                if has(q):
                    exp(turn, q, 2)
                if has(b):
                    high_part(kp, bank[2], 1, k_filled, k_high, kb_in, 32 * TERMS, turn, b)
                if has(q):
                    exp(turn, q, 3)
                if has(f):
                    wait_chunk(act, y2_filled, 1, turn, f - 1, 1)
                    copy(x2T[:], bank[1][:], x2T_filled, 1, turn, f, 1, x2T_taken)
                if has(q):
                    exp(turn, q, 4)
                    exp(turn, q, 5)
                    wait_chunk(act, otr_filled, 2, turn, q - 1, 1)
                    copy(oaug[:, 0, :], ps_o[:], o_filled, 2, turn, q, 1, o_taken)
                    exp(turn, q, 6)
                    exp(turn, q, 7)
                if has(f):
                    wait_chunk(act, gate_diff, 1, turn, f, 1)
                    nc.scalar.activation(gw[:, 1:2], gw[:, 0:1], ACT.Exp).then_inc(gate_exp, 1)
                if has(b):
                    wait_chunk(act, o_filled, 2, turn, b - 2, 2)
                    copy(vb[b % 2][0:64, :, :, 0:DH].rearrange("p b a d -> p (b a) d"),
                         bank[0][0:64, :].rearrange("p (m d) -> p m d", d=DH), v_filled, 1, turn, b, 1, v_low)
                if has(q):
                    wait_chunk(act, otr_filled, 2, turn, q - 1, 2)
                    copy(oaug[:, 1, :], ps_o[:], o_filled, 2, turn, q, 2, o_taken)
                    wait_chunk(act, y_filled, 1, turn, q - 1, 1)
                    copy(oT[:], bank[1][:], oT_filled, 1, turn, q, 1, oT_taken)
                if has(i):
                    wait_half(act, shift_in, 16, turn, i - 1)
                    copy(shiftT[:], bank[0][:, 0:64].bitcast(BF16), shiftT_filled, 1, turn, i, 1, shiftT_taken)
                if has(f):
                    wait_chunk(act, y2_filled, 1, turn, f - 1, 1)
                    for n in range(2):
                        copy(wmix[:, :, 64 * n:64 * n + 64].rearrange("p b (c h) -> p b c h", h=16),
                             bank[1 + n][:].rearrange("p (c b h) -> p b c h", b=CB, h=16),
                             wmix_filled, 2, turn, f, n + 1, wmix_taken)

            steps(act, step)

        @block.vector
        def _(dve):
            for n in range(2):
                nc.vector.memset(vb[n][:], 0.0).then_inc(vb_cleared, 1)
            dve.wait_ge(vb_cleared, 2)
            for n in range(2):
                for h2 in range(2):
                    nc.vector.memset(vb[n][64 * h2:64 * h2 + 64, :, :, 16 * h2 + DH:16 * h2 + DH + 1], 1.0).then_inc(vb_ones, 1)
            dve.wait_ge(w_in, 16 * 13)
            nc.vector.tensor_copy(bv_rep[:], bv_col[:].to_broadcast([P, P])).then_inc(set_dve, 1)
            dve.wait_ge(set_pe, 2)
            nc.vector.tensor_copy(wrT[:], bank[1][:, 0:EXPERTS]).then_inc(set_dve, 1)
            dve.wait_ge(set_pe, 3)
            nc.vector.tensor_copy(bwT[:].rearrange("p e d -> p (e d)"), bank[2][:]).then_inc(set_dve, 1)
            dve.wait_ge(set_act, 1)
            nc.vector.tensor_scalar(wo_g[:], wo[:], tg[:, 0:1], None, ALU.mult).then_inc(set_dve, 1)
            dve.wait_ge(set_pe, 4)
            nc.vector.tensor_scalar(c_rep[:], bank[0][:, 128:256], tg[:, 0:1], None, ALU.mult).then_inc(set_dve, 1)
            for n in range(2):
                dve.wait_ge(set_pe, 5 + n)
                nc.vector.tensor_scalar(mix_h[:, n:EXPERTS:2, :], bank[1 + n][:].rearrange("p (e d) -> p e d", d=D),
                                        tg[:, 1:2], None, ALU.mult).then_inc(set_dve, 2)
            for dst, src in ((wq_p, wq), (wk_p, wk)):
                nc.vector.tensor_copy(dst[:].rearrange("p (r a) -> p r a", a=PAIRS), src[:].rearrange("p (a r) -> p r a", a=PAIRS)).then_inc(set_dve, 1)
            nc.vector.tensor_copy(b_rowp[:].rearrange("p o (r a) -> p o r a", a=PAIRS),
                                  b_row[:].rearrange("p o (a r) -> p o r a", a=PAIRS)).then_inc(set_dve, 1)
            dve.wait_ge(set_pe, 7)
            nc.vector.tensor_copy(bias[:], bank[0][:, 256:258]).then_inc(set_dve, 1)

            def layer_norm(steps_sem, per, stats, work, src, turn, c):
                for t in range(TILES):
                    last = nc.vector.bn_stats(stats[:, t, :], src[:, t, :])
                last.then_inc(steps_sem, 1)
                wait_chunk(dve, steps_sem, per, turn, c, 1)
                nc.vector.tensor_tensor(work[:, 1, :], stats[:, :, 1], stats[:, :, 4], ALU.subtract).then_inc(steps_sem, 1)
                nc.vector.tensor_tensor(work[:, 2, :], stats[:, :, 2], stats[:, :, 5], ALU.add).then_inc(steps_sem, 1)
                nc.vector.tensor_tensor(work[:, 3, :], stats[:, :, 1], stats[:, :, 4], ALU.add).then_inc(steps_sem, 1)
                wait_chunk(dve, steps_sem, per, turn, c, 2)
                nc.vector.tensor_tensor(work[:, 4, :], work[:, 1, :], work[:, 1, :], ALU.mult).then_inc(steps_sem, 1)
                wait_chunk(dve, steps_sem, per, turn, c, 4)
                nc.vector.tensor_scalar(work[:, 0, :], work[:, 3, :], -0.5, None, ALU.mult).then_inc(steps_sem, 1)
                wait_chunk(dve, steps_sem, per, turn, c, 5)
                nc.vector.scalar_tensor_tensor(work[:, 2, :], work[:, 4, :], D / 4.0, work[:, 2, :],
                                               ALU.mult, ALU.add).then_inc(steps_sem, 1)
                wait_chunk(dve, steps_sem, per, turn, c, 7)
                nc.vector.tensor_scalar(work[:, 5, :], work[:, 2, :], 1.0 / D, EPS, ALU.mult, ALU.add).then_inc(steps_sem, 1)

            def parts(p, rest, src, col, high, taken, mid, low, turn, b):
                wait_chunk(dve, high, 1, turn, b, 1)
                wait_chunk(dve, low, 1, turn, b - 1, 1)
                nc.vector.scalar_tensor_tensor(rest[:], src[:], bias[:, col:col + 1], p[:, 0, :],
                                               ALU.add, ALU.subtract).then_inc(taken, 1)
                wait_chunk(dve, taken, 1, turn, b, 1)
                nc.vector.tensor_copy(p[:, 1, :], rest[:]).then_inc(mid, 1)

            def row_max(turn, i, fill):
                wait_chunk(dve, s_filled, PAIRS, turn, i, fill + 1)
                t, half = fill // 2, fill % 2
                nc.vector.tensor_reduce(nmax[:, :, 4 * half:4 * half + 4, t].rearrange("p g a -> p a g"),
                                        ps_s[fill % 2][:].rearrange("p (a g k) -> p a g k", g=2, k=SEQ),
                                        AX_X, ALU.max, negate=True).then_inc(s_max, 1)

            def normalise(turn, q, half):
                wait_chunk(dve, otr_filled, 2, turn, q, half + 1)
                blocks = bank[1 + half][:].rearrange("p (m w) -> p m w", w=16)
                nc.vector.reciprocal(rden[:, half, :], blocks[:, :, DH]).then_inc(rden_ready, 1)
                wait_chunk(dve, rden_ready, 2, turn, q, half + 1)
                wait_chunk(dve, oT_filled, 1, turn, q - 1, 1)
                nc.vector.tensor_tensor(o_tok[:, :, 64 * half:64 * half + 64].rearrange("p t (m d) -> p t m d", d=DH),
                                        blocks[:, :, 0:DH].rearrange("p (t m) d -> p t m d", t=TILES),
                                        rden[:, half, :].rearrange("p (t m o) -> p t m o", t=TILES, o=1).to_broadcast([P, TILES, 8, DH]),
                                        ALU.mult).then_inc(o_normed, 1)

            def top_two(turn, f):
                wait_chunk(dve, logit_filled, 1, turn, f, 1)
                nc.vector.tensor_copy(logit[:], bank[0][0:CB, 0:EXPERTS]).then_inc(gate_steps, 1)
                wait_chunk(dve, gate_steps, 8, turn, f, 1)
                dve.sem_inc(dve_waited, 1)
                nc.vector.max(top[:], logit[:]).then_inc(gate_steps, 1)
                wait_chunk(dve, gate_steps, 8, turn, f, 2)
                nc.vector.tensor_tensor(gw[:, 0:1], top[:, 1:2], top[:, 0:1], ALU.subtract).then_inc(gate_diff, 1)
                nc.vector.max_index(top_i[:], top[:], logit[:]).then_inc(gate_steps, 1)
                wait_chunk(dve, gate_steps, 8, turn, f, 3)
                nc.vector.tensor_copy(top_f[:], top_i[:]).then_inc(gate_steps, 1)

            def gate(turn, f):
                wait_chunk(dve, gate_exp, 1, turn, f, 1)
                nc.vector.tensor_scalar(gw[:, 2:3], gw[:, 1:2], 1.0, None, ALU.add).then_inc(gate_steps, 1)
                wait_chunk(dve, gate_steps, 8, turn, f, 5)
                nc.vector.reciprocal(gw[:, 3:4], gw[:, 2:3]).then_inc(gate_steps, 1)
                wait_chunk(dve, gate_steps, 8, turn, f, 6)
                nc.vector.tensor_tensor(gw[:, 4:5], gw[:, 1:2], gw[:, 3:4], ALU.mult).then_inc(gate_steps, 1)
                wait_chunk(dve, gate_steps, 8, turn, f, 7)
                nc.vector.tensor_scalar(gate_a[:], col_of[:], top_f[:, 0:1], gw[:, 3:4], ALU.is_equal, ALU.mult)
                nc.vector.tensor_scalar(gate_b[:], col_of[:], top_f[:, 1:2], gw[:, 4:5], ALU.is_equal, ALU.mult).then_inc(gate_steps, 1)
                wait_chunk(dve, gate_steps, 8, turn, f, 8)
                wait_chunk(dve, grep_filled, 1, turn, f - 1, 1)
                nc.vector.tensor_tensor(gates[:], gate_a[:, None, :].to_broadcast([CB, 16, EXPERTS]),
                                        gate_b[:, None, :].to_broadcast([CB, 16, EXPERTS]), ALU.add).then_inc(gates_ready, 1)

            def step(turn, i):
                a, b, q, f = i + 2, i + 1, i - 1, i - 2
                if i == -1:
                    dve.wait_ge(consts, 12)
                    dve.wait_ge(vb_ones, 4)
                if has(a):
                    wait_half(dve, x_in, 16, turn, a)
                    wait_chunk(dve, xn_ready, TILES, turn, a - 1, TILES)
                    layer_norm(ln1_steps, 8, stats1, work1, xt[a % 2], turn, a)
                if has(b):
                    parts(qp, q_rest, bank[1], 0, q_high, q_taken, q_mid, q_parts, turn, b)
                    parts(kp, k_rest, bank[2], 1, k_high, k_taken, k_mid, k_parts, turn, b)
                if has(f):
                    top_two(turn, f)
                    gate(turn, f)
                if has(i):
                    row_max(turn, i, 0)
                if has(b):
                    wait_chunk(dve, v_filled, 1, turn, b, 1)
                    wait_chunk(dve, o_filled, 2, turn, b - 2, 2)
                    wait_chunk(dve, v_low, 1, turn, b, 1)
                    nc.vector.tensor_copy(vb[b % 2][64:128, :, :, 16:16 + DH].rearrange("p b a d -> p (b a) d"),
                                          bank[0][64:128, :].rearrange("p (m d) -> p m d", d=DH)).then_inc(v_high, 1)
                if has(i):
                    row_max(turn, i, 1)
                if has(q):
                    normalise(turn, q, 0)
                if has(i):
                    row_max(turn, i, 2)
                if has(q):
                    normalise(turn, q, 1)
                if has(i):
                    row_max(turn, i, 3)
                if has(f):
                    wait_chunk(dve, grep_filled, 1, turn, f, 1)
                    wait_chunk(dve, wmix_filled, 2, turn, f - 1, 2)
                    nc.vector.tensor_tensor(gmix[:], bank[0][:, 0:CB].rearrange("p (b o) -> p b o", o=1).to_broadcast([P, CB, 16]),
                                            h16_mask[:, None, :].to_broadcast([P, CB, 16]), ALU.mult).then_inc(gmix_ready, 1)
                if has(i):
                    row_max(turn, i, 4)
                    row_max(turn, i, 5)
                if has(q):
                    wait_chunk(dve, y_filled, 1, turn, q, 1)
                    wait_chunk(dve, xr_ready, 1, turn, q, 1)
                    wait_half(dve, out_done, 16, turn, q - 2)
                    nc.vector.tensor_tensor(x1[q % 2][:].rearrange("p t d -> p (t d)"), bank[2][:],
                                            xr[q % 2][:].rearrange("p t d -> p (t d)"), ALU.add).then_inc(x1_ready, 1)
                if has(i):
                    row_max(turn, i, 6)
                    row_max(turn, i, 7)
                    wait_chunk(dve, s_max, PAIRS, turn, i, PAIRS)
                    wait_chunk(dve, shiftT_filled, 1, turn, i - 1, 1)
                    flat = nmax[:].rearrange("p g a t -> p (g a t)")
                    nc.vector.tensor_copy(shift[:, 0, :], flat).then_inc(shift_hi, 1)
                    wait_chunk(dve, shift_hi, 1, turn, i, 1)
                    nc.vector.tensor_tensor(shift[:, 1, :], flat, shift[:, 0, :], ALU.subtract).then_inc(shift_ready, 1)
                if has(q):
                    wait_chunk(dve, x1_ready, 1, turn, q, 1)
                    wait_chunk(dve, x1_scaled, TILES, turn, q - 1, TILES)
                    layer_norm(ln2_steps, 8, stats2, work2, x1[q % 2], turn, q)
                if has(f):
                    wait_chunk(dve, y2_filled, 1, turn, f, 1)
                    wait_chunk(dve, x1_scaled, TILES, turn, f, TILES)
                    flat = x1[f % 2][:].rearrange("p t d -> p (t d)")
                    nc.vector.tensor_tensor(flat, bank[0][:], flat, ALU.add).then_inc(out_ready, 1)

            steps(dve, step)

        @block.tensor
        def _(pe):
            mm = nc.tensor.matmul

            def tiles_T(dst, src):
                for t in range(TILES):
                    last = nc.tensor.transpose(dst[:, P * t:P * t + P], src[:, t, :], ident[:])
                return last

            pe.wait_ge(w_in, 16 * 13)
            pe.wait_ge(consts, 12)
            mm(bank[0][:, 0:2], ones_f[:], g_row[:], start=True, stop=True).then_inc(set_pe, 1)
            nc.tensor.transpose(bank[1][:, 0:EXPERTS], wr_in[:], ident[0:EXPERTS, 0:EXPERTS]).then_inc(set_pe, 1)
            for e4 in range(EXPERTS // 2):
                last = nc.tensor.transpose(bank[2][:, D * e4:D * e4 + D], bw_in[:, e4, :], ident[:])
            last.then_inc(set_pe, 1)
            pe.wait_ge(set_dve, 1)
            pe.wait_ge(set_act, 1)
            mm(bank[0][:, 128:256], bv_rep[:], wo[:], start=True, stop=False)
            mm(bank[0][:, 128:256], ones_f[:], bo_row[:], start=False, stop=True).then_inc(set_pe, 1)
            pe.wait_ge(set_dve, 3)
            for e in range(EXPERTS):
                e4, rows = e // 2, slice(RANK * (e % 2), RANK * (e % 2) + RANK)
                last = mm(bank[1 + e % 2][:, D * e4:D * e4 + D], bwT[rows, e4, :], a_in[rows, e4, :], start=True, stop=True)
                if e4 == 3:
                    last.then_inc(set_pe, 1)
            pe.wait_ge(set_dve, 12)
            for n in range(2):
                last = mm(bank[0][:, 256 + n:257 + n], b_rowp[:, n, :], ones_f[:, 0:1], start=True, stop=True)
            last.then_inc(set_pe, 1)
            pe.wait_ge(set_dve, 13)
            pe.wait_ge(vb_ones, 4)

            def key_scores(turn, q, pair):
                if pair == 0:
                    wait_half(pe, shift_in, 16, turn, q)
                wait_chunk(pe, t_exp, PAIRS, turn, q - (pair < 2), (pair - 2) % PAIRS + 1)
                n = q % 2
                for b in range(CB):
                    cols = slice(SEQ * b, SEQ * b + SEQ)
                    last = mm(ps_t[pair % 2][:, cols], kb[n][0:ROWS + SHIFT, pair, b, :, :], qa[n][0:ROWS + SHIFT, pair, cols],
                              start=True, stop=True)
                last.then_inc(t_filled, 1)

            def query_scores(turn, i, fill):
                wait_chunk(pe, s_max, PAIRS, turn, i - (fill < 2), (fill - 2) % PAIRS + 1)
                n, t = i % 2, fill // 2
                for a in range(4):
                    pair = 4 * (fill % 2) + a
                    for b2 in range(2):
                        cols = slice(P * t + SEQ * b2, P * t + SEQ * b2 + SEQ)
                        last = mm(ps_s[fill % 2][SEQ * b2:SEQ * b2 + SEQ, P * a:P * a + P], qa[n][0:ROWS, pair, cols],
                                  kb[n][0:ROWS, pair, 2 * t + b2, :, :], start=True, stop=True)
                last.then_inc(s_filled, 1)

            def times_v(turn, q, half):
                wait_chunk(pe, t_exp, PAIRS, turn, q, 4 * half + 4)
                wait_chunk(pe, o_taken, 2, turn, q - (half == 0), 2 - half)
                if half == 0:
                    wait_chunk(pe, v_low, 1, turn, q, 1)
                    wait_chunk(pe, v_high, 1, turn, q, 1)
                for b in range(CB):
                    cols = slice(SEQ * b, SEQ * b + SEQ)
                    for a in range(4):
                        last = mm(ps_o[VW * a:VW * a + VW, cols], vb[q % 2][:, b, 4 * half + a, :], prob[:, 4 * half + a, cols],
                                  start=True, stop=True, tile_position=(0, VW * a))
                last.then_inc(o_filled, 1)

            def o_back(turn, q, half):
                wait_chunk(pe, o_taken, 2, turn, q, half + 1)
                if half == 0:
                    if q > 0:
                        wait_chunk(pe, x2T_taken, 1, turn, q - 1, 1)
                    else:
                        wait_chunk(pe, q_taken, 1, turn, q + 2, 1)
                elif q < CHUNKS - 2:
                    wait_chunk(pe, k_taken, 1, turn, q + 2, 1)
                for t in range(TILES):
                    last = nc.tensor.transpose(bank[1 + half][:, P * t:P * t + P], oaug[:, half, P * t:P * t + P], ident[:])
                last.then_inc(otr_filled, 1)

            def step(turn, i):
                b, q, f = i + 1, i - 1, i - 2
                if has(b):
                    wait_chunk(pe, xn_ready, TILES, turn, b, TILES)
                    if b >= 4:
                        wait_chunk(pe, out_ready, 1, turn, b - 4, 1)
                    else:
                        wait_chunk(pe, shiftT_taken, 1, turn, b - 2, 1)
                        wait_chunk(pe, v_high, 1, turn, b - 1, 1)
                    tiles_T(bank[0], xn).then_inc(xnT_filled, 1)
                    wait_half(pe, c_in, 16, turn, b)
                    if b >= 4:
                        wait_chunk(pe, wmix_taken, 2, turn, b - 4, 1)
                    else:
                        wait_chunk(pe, oT_taken, 1, turn, b - 3, 1)
                        wait_chunk(pe, q_taken, 1, turn, b - 1, 1)
                    tiles_T(bank[1], ct[b % 2]).then_inc(cT_filled, 1)
                if has(q):
                    key_scores(turn, q, 0)
                    key_scores(turn, q, 1)
                if has(b):
                    wait_chunk(pe, xnT_taken, 1, turn, b, 1)
                    wait_chunk(pe, cT_taken, 1, turn, b, 1)
                    mm(bank[1][:], wq_p[:], xnT[:], start=True, stop=True).then_inc(q_filled, 1)
                if has(q):
                    key_scores(turn, q, 2)
                if has(b):
                    if b >= 4:
                        wait_chunk(pe, wmix_taken, 2, turn, b - 4, 2)
                    else:
                        wait_chunk(pe, x1_ready, 1, turn, b - 3, 1)
                        wait_chunk(pe, k_taken, 1, turn, b - 1, 1)
                    mm(bank[2][:], wk_p[:], cT[:], start=True, stop=True).then_inc(k_filled, 1)
                if has(q):
                    key_scores(turn, q, 3)
                if has(f):
                    wait_chunk(pe, xn2_ready, TILES, turn, f, TILES)
                    wait_chunk(pe, wmix_taken, 2, turn, f - 1, 2)
                    if f < CHUNKS - 3:
                        wait_chunk(pe, q_taken, 1, turn, f + 3, 1)
                    tiles_T(bank[1], xn2).then_inc(x2T_filled, 1)
                if has(q):
                    key_scores(turn, q, 4)
                    key_scores(turn, q, 5)
                    times_v(turn, q, 0)
                if has(f):
                    wait_chunk(pe, x2T_taken, 1, turn, f, 1)
                    wait_chunk(pe, out_ready, 1, turn, f - 1, 1)
                    mm(bank[0][0:CB, 0:EXPERTS], x2T[:, 0:TOK:SEQ], wrT[:], start=True, stop=True).then_inc(logit_filled, 1)
                if has(q):
                    key_scores(turn, q, 6)
                    key_scores(turn, q, 7)
                if has(b):
                    wait_chunk(pe, xnT_taken, 1, turn, b, 1)
                    wait_chunk(pe, gate_steps, 8, turn, b - 3, 1)
                    for bb in range(CB):
                        for h2 in range(2):
                            last = mm(bank[0][64 * h2:64 * h2 + 64, 64 * bb:64 * bb + 64], cT[:, SEQ * bb:SEQ * bb + SEQ],
                                      wv[:].rearrange("p (a g d) -> p g a d", g=2, d=DH)[:, h2], start=True, stop=True)
                    last.then_inc(v_filled, 1)
                if has(i):
                    wait_half(pe, qa_in, 16 * TERMS, turn, i)
                    wait_half(pe, kb_in, 32 * TERMS, turn, i)
                    query_scores(turn, i, 0)
                if has(q):
                    times_v(turn, q, 1)
                if has(i):
                    query_scores(turn, i, 1)
                if has(q):
                    o_back(turn, q, 0)
                if has(i):
                    query_scores(turn, i, 2)
                if has(q):
                    o_back(turn, q, 1)
                if has(i):
                    query_scores(turn, i, 3)
                if has(f):
                    wait_chunk(pe, gates_ready, 1, turn, f, 1)
                    if f < CHUNKS - 3:
                        wait_chunk(pe, v_high, 1, turn, f + 3, 1)
                    mm(bank[0][:, 0:CB], gates[:].rearrange("b h e -> b (h e)"), ident[0:CB, 0:CB],
                       start=True, stop=True).then_inc(grep_filled, 1)
                if has(i):
                    query_scores(turn, i, 4)
                if has(q):
                    wait_chunk(pe, o_normed, 2, turn, q, 2)
                    tiles_T(bank[1], o_tok).then_inc(oT_filled, 1)
                if has(i):
                    query_scores(turn, i, 5)
                if has(q):
                    wait_chunk(pe, oT_taken, 1, turn, q, 1)
                    for t in range(TILES):
                        last = mm(bank[2][:, D * t:D * t + D], oT[:, P * t:P * t + P], wo_g[:], start=True, stop=True)
                    last.then_inc(y_filled, 1)
                if has(i):
                    query_scores(turn, i, 6)
                    query_scores(turn, i, 7)
                def mix_half(n):
                    for hc in range(4):
                        last = mm(bank[1 + n][:, P * hc:P * hc + P], mix[:, 4 * n + hc, :], gmix[:].rearrange("p b h -> p (b h)"),
                                  start=True, stop=True)
                    last.then_inc(wmix_filled, 1)
                if has(f):
                    if f == 0:
                        pe.wait_ge(mix_in, 16 * HC)
                    wait_chunk(pe, gmix_ready, 1, turn, f, 1)
                    if f < CHUNKS - 1:
                        wait_chunk(pe, oT_taken, 1, turn, f + 1, 1)
                    mix_half(0)
                if has(i):
                    wait_chunk(pe, shift_ready, 1, turn, i, 1)
                    if has(f):
                        wait_chunk(pe, gmix_ready, 1, turn, f, 1)
                    if has(b):
                        wait_chunk(pe, v_high, 1, turn, b, 1)
                    nc.tensor.transpose(bank[0][:, 0:64].bitcast(BF16), shift[:].rearrange("p h m -> p (h m)"), identb[:]).then_inc(shiftT_filled, 1)
                if has(f):
                    if f < CHUNKS - 1:
                        wait_chunk(pe, x1_ready, 1, turn, f + 1, 1)
                    mix_half(1)
                    if f < CHUNKS - 2:
                        wait_chunk(pe, shiftT_taken, 1, turn, f + 2, 1)
                    wait_chunk(pe, wmix_taken, 2, turn, f, 2)
                    for bb in range(CB):
                        rows = slice(64 * (bb % 2), 64 * (bb % 2) + 64)
                        last = mm(bank[0][rows, D * (bb // 2):D * (bb // 2) + D], x2T[:, SEQ * bb:SEQ * bb + SEQ], wmix[:, bb, :],
                                  start=True, stop=True)
                    last.then_inc(y2_filled, 1)

            steps(pe, step)


_INS = ['x', 'ctx_1024', 'g_xattn', 'g_ffn', 'L0_xattn_Wq', 'L0_xattn_bq', 'L0_xattn_Wk', 'L0_xattn_bk', 'L0_xattn_Wv',
        'L0_xattn_bv', 'L0_xattn_Wo', 'L0_xattn_bo', 'L0_ffn_Wr', 'L0_ffn_A', 'L0_ffn_Bw']


def kernel(**inputs):
    import numpy as _np
    import concourse.bacc as _bacc
    from concourse import mybir as _mybir
    from concourse.bass_utils import run_bass_kernel_spmd as _run

    nc = _bacc.Bacc("TRN2", target_bir_lowering=False, num_devices=1)
    arrays, args = {}, []
    for name in _INS:
        a = _np.ascontiguousarray(inputs[name])
        arrays[f"in_{name}_dram"] = a
        args.append(nc.dram_tensor(f"in_{name}_dram", a.shape, _mybir.dt.from_np(a.dtype), kind="ExternalInput").ap())
    args.append(nc.dram_tensor("out_0_dram", (BATCHES, SEQ, D), _mybir.dt.float32, kind="ExternalOutput").ap())
    block_attention_experts(nc, *args)
    r = _run(nc, [arrays], core_ids=[0])
    return r.results[0]["out_0_dram"]
```

```python
from contextlib import ExitStack

import concourse.bass as bass
from concourse import mybir

P = 128
BATCHES, SEQ, D = 128, 64, 128
HEADS, DH = 16, 8
PAIRS = HEADS // 2
EXPERTS, RANK = 8, 64
CB = 8
CHUNKS = BATCHES // CB
TOK = CB * SEQ
TILES = TOK // P
Q_PART = (0, 1, 2, 0, 1, 0)
K_PART = (0, 0, 0, 1, 1, 2)
TERMS = len(Q_PART)
ROWS = TERMS * 2 * DH
SHIFT = 4
VW = 32
HC = D // 16
EPS = 1e-5

ALU = mybir.AluOpType
ACT = mybir.ActivationFunctionType
BF16 = mybir.dt.bfloat16
F32 = mybir.dt.float32
U32 = mybir.dt.uint32
AX_X = mybir.AxisListType.X

FIRST, LAST = -4, CHUNKS + 1
LOOP_FIRST = 3
LOOP_TURNS = (CHUNKS - 4 - LOOP_FIRST) // 2
LOOP_END = LOOP_FIRST + 2 * LOOP_TURNS


def block_attention_experts(nc, x, ctx_in, g_xattn, g_ffn, Wq, bq, Wk, bk, Wv, bv, Wo, bo, Wr, A, Bw, out):
    x_v = x.rearrange("(c t b) s d -> c (b s) t d", t=TILES, b=2)
    c_v = ctx_in.rearrange("(c t b) s d -> c (b s) t d", t=TILES, b=2)
    o_v = out.rearrange("(c t b) s d -> c (b s) t d", t=TILES, b=2)

    stack = ExitStack()
    with stack:
        def sb(name, shape, dt=F32):
            return stack.enter_context(nc.sbuf_tensor(name, shape, dt))

        def pb(name, shape, dt=F32):
            return stack.enter_context(nc.psum_tensor(name, shape, dt))

        def sem(name):
            return stack.enter_context(nc.semaphore(name))

        def two(make, name, shape, dt=F32):
            return [make(f"{name}{n}", shape, dt) for n in range(2)]

        ident = sb("ident", [P, P])
        identb = sb("identb", [P, P], BF16)
        ones_f = sb("ones_f", [1, P])
        one_f = sb("one_f", [P, 1])
        minus_half = sb("minus_half", [P, TILES])
        ones_b = sb("ones_b", [2 * PAIRS, TOK], BF16)
        col_of = sb("col_of", [CB, EXPERTS])
        h16_mask = sb("h16_mask", [P, 16])
        wq, wk, wv, wo, wo_g = (sb(n, [P, D]) for n in ("wq", "wk", "wv", "wo", "wo_g"))
        wq_p, wk_p = sb("wq_p", [P, D]), sb("wk_p", [P, D])
        b_row = sb("b_row", [1, 2, D])
        b_rowp = sb("b_rowp", [1, 2, D])
        bias = sb("bias", [P, 2])
        bv_col = sb("bv_col", [P, 1])
        bo_row = sb("bo_row", [1, D])
        bv_rep = sb("bv_rep", [P, P])
        g_row = sb("g_row", [1, 2])
        tg = sb("tg", [P, 2])
        c_rep = sb("c_rep", [P, D])
        wr_in = sb("wr_in", [EXPERTS, D])
        wrT = sb("wrT", [D, EXPERTS])
        a_in = sb("a_in", [P, EXPERTS // 2, D])
        bw_in = sb("bw_in", [D, EXPERTS // 2, P])
        bwT = sb("bwT", [P, EXPERTS // 2, D])
        mix_h = sb("mix_h", [P, EXPERTS, D])
        mix = sb("mix", [P, HC, D])

        xt = two(sb, "xt", [P, TILES, D])
        ct = two(sb, "ct", [P, TILES, D])
        stats1 = sb("stats1", [P, TILES, 6])
        mean_var1 = sb("mean_var1", [P, TILES, 2])
        norm1 = sb("norm1", [P, 4, TILES])
        stats2 = sb("stats2", [P, TILES, 6])
        mean_var2 = sb("mean_var2", [P, TILES, 2])
        norm2 = sb("norm2", [P, 6, TILES])
        xn = sb("xn", [P, TILES, D])
        xnT = sb("xnT", [D, TOK])
        cT = two(sb, "cT", [D, TOK])
        qp = two(sb, "qp", [P, 3, TOK], BF16)
        kp = two(sb, "kp", [P, 3, TOK], BF16)
        q_rest = sb("q_rest", [P, TOK])
        k_rest = sb("k_rest", [P, TOK])
        qa = two(sb, "qa", [P, PAIRS, TOK], BF16)
        kb = two(sb, "kb", [P, PAIRS, CB, 2, SEQ], BF16)
        vb = two(sb, "vb", [P, CB, PAIRS, VW])
        nmax = sb("nmax", [P, 2, PAIRS, TILES])
        shift = sb("shift", [P, 2, 2, PAIRS * TILES], BF16)
        shiftT = sb("shiftT", [P, P], BF16)
        prob = sb("prob", [P, PAIRS, TOK])
        oaug = sb("oaug", [P, 2, TOK])
        rden = sb("rden", [P, 2, 32])
        o_tok = sb("o_tok", [P, TILES, D])
        oT = sb("oT", [D, TOK])
        xr = two(sb, "xr", [P, TILES, D])
        x1 = two(sb, "x1", [P, TILES, D])
        xn2 = sb("xn2", [P, TILES, D])
        x2T = sb("x2T", [D, TOK])
        logit = sb("logit", [CB, EXPERTS])
        top = sb("top", [CB, EXPERTS])
        top_i = sb("top_i", [CB, EXPERTS], U32)
        top_f = sb("top_f", [CB, EXPERTS])
        gw = sb("gw", [CB, 6])
        gate_a = sb("gate_a", [CB, EXPERTS])
        gate_b = sb("gate_b", [CB, EXPERTS])
        gates = sb("gates", [CB, 16, EXPERTS])
        gmix = sb("gmix", [P, CB, 16])
        wmix = sb("wmix", [D, CB, D])

        ps_s = two(pb, "ps_s", [P, TOK])
        ps_t = two(pb, "ps_t", [P, TOK])
        ps_o = pb("ps_o", [P, TOK])
        bank = [pb(f"bank{n}", [P, TOK]) for n in range(3)]

        w_qk_in, w_in = sem("w_qk_in"), sem("w_in")
        pool_waited, dve_waited, sp_waited = sem("pool_waited"), sem("dve_waited"), sem("sp_waited")
        mix_in = sem("mix_in")
        kb_ones = [sem(f"kb_ones{n}") for n in range(2)]
        consts, ones_ready = sem("consts"), sem("ones_ready")
        qk_cols, bias_filled, bias_ready = sem("qk_cols"), sem("bias_filled"), sem("bias_ready")
        kb_cleared, vb_cleared, vb_ones = sem("kb_cleared"), sem("vb_cleared"), sem("vb_ones")
        set_pe = sem("set_pe")
        set_dve = sem("set_dve")
        set_act = sem("set_act")
        x_in = [sem(f"x_in{n}") for n in range(2)]
        c_in = [sem(f"c_in{n}") for n in range(2)]
        xr_in = [sem(f"xr_in{n}") for n in range(2)]
        qa_in = [sem(f"qa_in{n}") for n in range(2)]
        kb_in = [sem(f"kb_in{n}") for n in range(2)]
        shift_in = [sem(f"shift_in{n}") for n in range(2)]
        out_done = [sem(f"out_done{n}") for n in range(2)]
        ln1_steps = sem("ln1_steps")
        ln2_steps = sem("ln2_steps")
        rstd1_ready, rstd2_ready = sem("rstd1_ready"), sem("rstd2_ready")
        xn_ready = sem("xn_ready")
        xnT_filled, xnT_taken = sem("xnT_filled"), sem("xnT_taken")
        cT_filled, cT_taken = sem("cT_filled"), sem("cT_taken")
        q_filled, q_high, q_taken, q_mid, q_parts = (sem(n) for n in ("q_filled", "q_high", "q_taken", "q_mid", "q_parts"))
        k_filled, k_high, k_taken, k_mid, k_parts = (sem(n) for n in ("k_filled", "k_high", "k_taken", "k_mid", "k_parts"))
        v_filled, v_taken = sem("v_filled"), sem("v_taken")
        s_filled, s_max = sem("s_filled"), sem("s_max")
        shift_hi, shift_ready = sem("shift_hi"), sem("shift_ready")
        shiftT_filled, shiftT_taken = sem("shiftT_filled"), sem("shiftT_taken")
        t_filled, t_exp = sem("t_filled"), sem("t_exp")
        o_filled, o_taken = sem("o_filled"), sem("o_taken")
        otr_filled, rden_ready, o_normed = sem("otr_filled"), sem("rden_ready"), sem("o_normed")
        oT_filled, oT_taken = sem("oT_filled"), sem("oT_taken")
        xr_ready = sem("xr_ready")
        y_filled, x1_ready = sem("y_filled"), sem("x1_ready")
        xn2_ready, x1_scaled = sem("xn2_ready"), sem("x1_scaled")
        x2T_filled, x2T_taken = sem("x2T_filled"), sem("x2T_taken")
        logit_filled, gate_steps, gate_diff, gate_exp, gates_ready = (
            sem(n) for n in ("logit_filled", "gate_steps", "gate_diff", "gate_exp", "gates_ready"))
        grep_filled, gmix_ready = sem("grep_filled"), sem("gmix_ready")
        wmix_filled, wmix_taken = sem("wmix_filled"), sem("wmix_taken")
        y2_filled, out_ready = sem("y2_filled"), sem("out_ready")

        block = stack.enter_context(nc.Block())

        def steps(eng, step):
            for i in range(FIRST, LOOP_FIRST):
                step(0, i)
            with eng.Fori(0, LOOP_TURNS) as turn:
                step(turn, LOOP_FIRST)
                step(turn, LOOP_FIRST + 1)
            for i in range(LOOP_END, LAST + 1):
                step(0, i)

        def has(c):
            return 0 <= c < CHUNKS

        def wait_chunk(eng, s, per, turn, c, n):
            if per * c + n > 0 and c >= 0:
                eng.wait_ge(s, 2 * per * turn + (per * c + n))

        def wait_half(eng, pair_of_sems, per, turn, c):
            if c >= 0:
                eng.wait_ge(pair_of_sems[c % 2], per * turn + per * (c // 2 + 1))

        @block.sync
        def _(sp):
            def load_qk_weights():
                for dst, src in ((wq[:], Wq), (b_row[:, 0, :], bq.rearrange("(o n) -> o n", o=1)),
                                 (b_row[:, 1, :], bk.rearrange("(o n) -> o n", o=1)), (wk[:], Wk)):
                    sp.dma_start(dst, src).then_inc(w_qk_in, 16)

            def load_weights():
                for dst, src in ((wv[:], Wv), (wo[:], Wo),
                                 (bv_col[:], bv.rearrange("(p o) -> p o", o=1)),
                                 (bo_row[:], bo.rearrange("(o n) -> o n", o=1)),
                                 (g_row[:, 0:1], g_xattn.rearrange("(o n) -> o n", o=1)),
                                 (g_row[:, 1:2], g_ffn.rearrange("(o n) -> o n", o=1)),
                                 (wr_in[:], Wr),
                                 (a_in[:], A.rearrange("(e4 e2) r d -> (e2 r) e4 d", e2=2)),
                                 (bw_in[:].rearrange("h e4 (e2 r) -> h (e4 e2) r", e2=2), Bw.rearrange("e h r -> h e r"))):
                    sp.dma_start(dst, src).then_inc(w_in, 16)

            def lay_ones(n):
                sp.wait_ge(ones_ready, 1)
                sp.wait_ge(kb_cleared, n + 1)
                for h2 in range(2):
                    row = ROWS + 2 * h2
                    sp.dma_start(kb[n][row:row + 2, :, :, h2, :], ones_b[:, :]).then_inc(kb_ones[n], 16)

            def spread_mix():
                sp.wait_ge(set_dve, 7)
                for hc in range(HC):
                    sp.dma_start(mix[:, hc, :], mix_h[16 * hc:16 * hc + 16, :, :]).then_inc(mix_in, 16)

            def step(turn, i):
                l, v, f = i + 4, i + 1, i - 2

                def load_x():
                    source = x_v[bass.ds(2 * turn + l, 1)].rearrange("o p t d -> p (o t) d")
                    wait_chunk(sp, xn_ready, TILES, turn, l - 2, TILES)
                    sp.dma_start(xt[l % 2][:], source).then_inc(x_in[l % 2], 16)

                if l in (0, 1):
                    load_x()
                if l in (0, 1):
                    sp.dma_start(ct[l][:], c_v[bass.ds(l, 1)].rearrange("o p t d -> p (o t) d")).then_inc(c_in[l], 16)
                if l == 0:
                    load_qk_weights()
                if l == 1:
                    load_weights()
                if has(i):
                    wait_chunk(sp, x1_ready, 1, turn, i - 2, 1)
                    sp.dma_start(xr[i % 2][:], x_v[bass.ds(2 * turn + i, 1)].rearrange("o p t d -> p (o t) d")).then_inc(xr_in[i % 2], 16)
                if has(v):
                    n = v % 2
                    if v < 2:
                        lay_ones(v)
                    if v >= 2:
                        wait_chunk(sp, t_filled, PAIRS, turn, v - 2, PAIRS)
                        sp.sem_inc(sp_waited, 1)
                    for part, q_ready, k_ready in ((0, q_high, k_high), (1, q_mid, k_mid), (2, q_parts, k_parts)):
                        wait_chunk(sp, q_ready, 1, turn, v, 1)
                        for t in range(TERMS):
                            if Q_PART[t] == part:
                                sp.dma_start(qa[n][16 * t:16 * t + 16, :, :], qp[n][:, part, :]).then_inc(qa_in[n], 16)
                        wait_chunk(sp, k_ready, 1, turn, v, 1)
                        for t in range(TERMS):
                            for h2 in range(2):
                                if K_PART[t] == part:
                                    r = 16 * t + 8 * h2
                                    sp.dma_start(kb[n][r:r + DH, :, :, h2, :], kp[n][64 * h2:64 * h2 + 64, part, :]).then_inc(kb_in[n], 16)
                if has(l) and l >= 2:
                    load_x()
                if i == 0:
                    spread_mix()
                if has(l) and l >= 2:
                    source = c_v[bass.ds(2 * turn + l, 1)].rearrange("o p t d -> p (o t) d")
                    wait_chunk(sp, cT_filled, 1, turn, l - 2, 1)
                    sp.dma_start(ct[l % 2][:], source).then_inc(c_in[l % 2], 16)
                if has(f):
                    wait_chunk(sp, out_ready, 1, turn, f, 1)
                    sp.dma_start(o_v[bass.ds(2 * turn + f, 1)].rearrange("o p t d -> p (o t) d"), x1[f % 2][:]).then_inc(out_done[f % 2], 16)

            steps(sp, step)
            for n in range(2):
                sp.wait_ge(out_done[n], 16 * CHUNKS // 2)

        @block.gpsimd
        def _(pool):
            pool.memset(ident[:], 0.0).then_inc(consts, 1)
            pool.memset(identb[:], 0.0).then_inc(consts, 1)
            pool.memset(h16_mask[:], 1.0).then_inc(consts, 1)
            pool.memset(ones_b[:], 1.0).then_inc(ones_ready, 1)
            pool.memset(minus_half[:], -0.5).then_inc(consts, 1)
            pool.memset(ones_f[:], 1.0).then_inc(consts, 1)
            pool.memset(one_f[:], 1.0).then_inc(consts, 1)
            pool.iota(top_i[:], [[1, EXPERTS]], base=0, channel_multiplier=0).then_inc(consts, 1)
            pool.wait_ge(consts, 7)
            pool.tensor_copy(col_of[:], top_i[:]).then_inc(consts, 1)
            for m in (ident, identb):
                pool.affine_select(out=m[:], in_=m[:], compare_op=ALU.not_equal, fill=1.0,
                                   base=0, pattern=[[-1, P]], channel_multiplier=1).then_inc(consts, 1)
            pool.affine_select(out=h16_mask[:], in_=h16_mask[:], compare_op=ALU.is_ge, fill=0.0,
                               base=0, pattern=[[-8, 16]], channel_multiplier=1).then_inc(consts, 1)
            pool.wait_ge(consts, 11)
            pool.affine_select(out=h16_mask[:], in_=h16_mask[:], compare_op=ALU.is_ge, fill=0.0,
                               base=7, pattern=[[8, 16]], channel_multiplier=-1).then_inc(consts, 1)

            def clear_kb(n):
                pool.memset(kb[n][:].rearrange("p a b g k -> p (a b g k)").bitcast(F32), 0.0).then_inc(kb_cleared, 1)

            def rstd(stats_sem, norm, done, n, turn, c):
                wait_chunk(pool, stats_sem, 4, turn, c, 4)
                pool.tensor_tensor(norm[:, 2, :], norm[:, 1, :], minus_half[:], ALU.pow).then_inc(done, 1)
                wait_chunk(pool, done, n, turn, c, 1)
                pool.tensor_tensor(norm[:, 3, :], norm[:, 0, :], norm[:, 2, :], ALU.mult).then_inc(done, 1)

            def low_part(ready, p, rest, done, turn, b):
                wait_chunk(pool, ready, 1, turn, b, 1)
                pool.tensor_tensor(p[:, 2, :], rest[:], p[:, 1, :], ALU.subtract).then_inc(done, 1)

            def step(turn, i):
                b, q, f = i + 2, i - 1, i - 2
                if has(b):
                    rstd(ln1_steps, norm1, rstd1_ready, 2, turn, b)
                if has(f):
                    rstd(ln2_steps, norm2, rstd2_ready, 4, turn, f)
                    wait_chunk(pool, rstd2_ready, 4, turn, f, 2)
                    wait_chunk(pool, x2T_filled, 1, turn, f - 1, 1)
                    pool.sem_inc(pool_waited, 1)
                    for t in range(TILES):
                        pool.tensor_scalar(xn2[:, t, :], x1[f % 2][:, t, :], norm2[:, 2, t:t + 1], norm2[:, 3, t:t + 1],
                                           ALU.mult, ALU.add).then_inc(xn2_ready, 1)
                if has(b):
                    wait_chunk(pool, rstd1_ready, 2, turn, b, 2)
                    wait_chunk(pool, xnT_filled, 1, turn, b - 1, 1)
                    wait_half(pool, x_in, 16, turn, b)
                    pool.sem_inc(pool_waited, 1)
                    for t in range(TILES):
                        pool.tensor_scalar(xn[:, t, :], xt[b % 2][:, t, :], norm1[:, 2, t:t + 1], norm1[:, 3, t:t + 1],
                                           ALU.mult, ALU.add).then_inc(xn_ready, 1)
                if i == -2:
                    clear_kb(0)
                if has(q):
                    if q == 0:
                        pool.wait_ge(set_dve, 5)
                    wait_half(pool, xr_in, 16, turn, q)
                    pool.tensor_tensor(xr[q % 2][:], xr[q % 2][:], c_rep[:, None, :].to_broadcast([P, TILES, D]),
                                       ALU.add).then_inc(xr_ready, 1)
                if has(f):
                    pool.tensor_scalar(norm2[:, 4, :], norm2[:, 2, :], tg[:, 1:2], one_f[:, 0:1], ALU.mult, ALU.add).then_inc(rstd2_ready, 1)
                    pool.tensor_scalar(norm2[:, 5, :], norm2[:, 3, :], tg[:, 1:2], None, ALU.mult).then_inc(rstd2_ready, 1)
                    wait_chunk(pool, rstd2_ready, 4, turn, f, 4)
                    wait_chunk(pool, xn2_ready, TILES, turn, f, TILES)
                    pool.sem_inc(pool_waited, 1)
                    for t in range(TILES):
                        pool.tensor_scalar(x1[f % 2][:, t, :], x1[f % 2][:, t, :], norm2[:, 4, t:t + 1], norm2[:, 5, t:t + 1],
                                           ALU.mult, ALU.add).then_inc(x1_scaled, 1)
                if has(i):
                    wait_chunk(pool, shiftT_taken, 1, turn, i, 1)
                    pool.sem_inc(pool_waited, 1)
                    pool.dma_start(qa[i % 2][ROWS:ROWS + SHIFT, :, :].rearrange("r a n -> r (a n)"), shiftT[:, :]).then_inc(shift_in[i % 2], 16)
                if has(b):
                    low_part(q_mid, qp[b % 2], q_rest, q_parts, turn, b)
                    low_part(k_mid, kp[b % 2], k_rest, k_parts, turn, b)
                if i == -1:
                    clear_kb(1)

            steps(pool, step)

        @block.scalar
        def _(act):
            def copy(dst, src, filled, per, turn, c, n, done):
                wait_chunk(act, filled, per, turn, c, n)
                nc.scalar.activation(dst, src, ACT.Copy).then_inc(done, 1)

            def high_part(p, src, col, filled, high, landed, per, turn, b):
                wait_half(act, landed, per, turn, b - 2)
                wait_chunk(act, filled, 1, turn, b, 1)
                nc.scalar.activation(p[:, 0, :], src[:], ACT.Identity, bias=bias[:, col:col + 1]).then_inc(high, 1)

            def middle_part(p, rest, taken, mid, turn, b):
                wait_chunk(act, taken, 1, turn, b, 1)
                nc.scalar.activation(p[:, 1, :], rest[:], ACT.Copy).then_inc(mid, 1)

            def mixed(turn, f, n):
                copy(wmix[:, :, 64 * n:64 * n + 64].rearrange("p b (c h) -> p b c h", h=16),
                     ps_s[n][:].rearrange("p (c b h) -> p b c h", b=CB, h=16),
                     wmix_filled, 2, turn, f, n + 1, wmix_taken)

            def exp(turn, q, pair):
                wait_chunk(act, t_filled, PAIRS, turn, q, pair + 1)
                wait_chunk(act, o_filled, 2, turn, q - 1, pair // 4 + 1)
                nc.scalar.activation(prob[:, pair, :], ps_t[pair % 2][:], ACT.Exp, scale=DH ** -0.5).then_inc(t_exp, 1)

            def step(turn, i):
                b, v, q, f = i + 2, i + 1, i - 1, i - 2
                if has(q):
                    for pair in range(PAIRS):
                        exp(turn, q, pair)
                    wait_chunk(act, otr_filled, 2, turn, q - 1, 1)
                    copy(oaug[:, 0, :], ps_o[:], o_filled, 2, turn, q, 1, o_taken)
                if has(f):
                    wait_chunk(act, y2_filled, 1, turn, f - 1, 1)
                    copy(x2T[:], bank[2][:], x2T_filled, 1, turn, f, 1, x2T_taken)
                    wait_chunk(act, gate_diff, 1, turn, f, 1)
                    nc.scalar.activation(gw[:, 1:2], gw[:, 0:1], ACT.Exp).then_inc(gate_exp, 1)
                if has(q):
                    wait_chunk(act, otr_filled, 2, turn, q - 1, 2)
                    copy(oaug[:, 1, :], ps_o[:], o_filled, 2, turn, q, 2, o_taken)
                if has(b):
                    wait_chunk(act, q_filled, 1, turn, b - 1, 1)
                    copy(xnT[:], ps_t[0][:], xnT_filled, 1, turn, b, 1, xnT_taken)
                    wait_chunk(act, v_filled, 1, turn, b - 2, 1)
                    copy(cT[b % 2][:], ps_t[1][:], cT_filled, 1, turn, b, 1, cT_taken)

                def value_half(h2):
                    copy(vb[v % 2][64 * h2:64 * h2 + 64, :, :, 16 * h2:16 * h2 + DH].rearrange("p b a d -> p (b a) d"),
                         bank[0][64 * h2:64 * h2 + 64, :].rearrange("p (m d) -> p m d", d=DH), v_filled, 1, turn, v, 1, v_taken)

                def shift_rows():
                    wait_half(act, shift_in, 16, turn, i - 1)
                    copy(shiftT[:], bank[2][:, 0:64].bitcast(BF16), shiftT_filled, 1, turn, i, 1, shiftT_taken)

                if i == 0:
                    shift_rows()
                if has(b):
                    if b == 0:
                        act.wait_ge(bias_ready, 1)
                    high_part(qp[b % 2], ps_t[0], 0, q_filled, q_high, qa_in, 16 * TERMS, turn, b)
                if has(v):
                    if v == 0:
                        act.wait_ge(vb_ones, 4)
                    wait_chunk(act, o_filled, 2, turn, v - 2, 2)
                    value_half(0)
                if has(i) and i > 0:
                    shift_rows()
                if has(b):
                    high_part(kp[b % 2], ps_t[1], 1, k_filled, k_high, kb_in, 32 * TERMS, turn, b)
                if has(v):
                    value_half(1)
                if has(f):
                    mixed(turn, f, 0)
                    mixed(turn, f, 1)
                if has(q):
                    wait_chunk(act, y_filled, 1, turn, q - 1, 1)
                    copy(oT[:], bank[0][:], oT_filled, 1, turn, q, 1, oT_taken)
                if has(b):
                    middle_part(qp[b % 2], q_rest, q_taken, q_mid, turn, b)
                    middle_part(kp[b % 2], k_rest, k_taken, k_mid, turn, b)
                if i == -2:
                    act.wait_ge(set_pe, 1)
                    nc.scalar.activation(tg[:], ps_s[0][:, 0:2], ACT.Tanh).then_inc(set_act, 1)

            steps(act, step)

        @block.vector
        def _(dve):
            def clear_vb(n):
                nc.vector.memset(vb[n][:], 0.0).then_inc(vb_cleared, 1)
                dve.wait_ge(vb_cleared, n + 1)
                for h2 in range(2):
                    nc.vector.memset(vb[n][64 * h2:64 * h2 + 64, :, :, 16 * h2 + DH:16 * h2 + DH + 1], 1.0).then_inc(vb_ones, 1)

            def order_qk():
                dve.wait_ge(w_qk_in, 16 * 4)
                nc.vector.tensor_copy(b_rowp[:].rearrange("p o (r a) -> p o r a", a=PAIRS),
                                      b_row[:].rearrange("p o (a r) -> p o r a", a=PAIRS)).then_inc(qk_cols, 1)
                for dst, src in ((wq_p, wq), (wk_p, wk)):
                    nc.vector.tensor_copy(dst[:].rearrange("p (r a) -> p r a", a=PAIRS), src[:].rearrange("p (a r) -> p r a", a=PAIRS)).then_inc(qk_cols, 1)
                dve.wait_ge(bias_filled, 1)
                nc.vector.tensor_copy(bias[:], bank[0][:, 0:2]).then_inc(bias_ready, 1)

            def set_up():
                dve.wait_ge(w_in, 16 * 9)
                nc.vector.tensor_copy(bv_rep[:], bv_col[:].to_broadcast([P, P])).then_inc(set_dve, 1)
                dve.wait_ge(set_pe, 2)
                nc.vector.tensor_copy(wrT[:], ps_s[1][:, 0:EXPERTS]).then_inc(set_dve, 1)
                dve.wait_ge(set_pe, 3)
                nc.vector.tensor_copy(bwT[:].rearrange("p e d -> p (e d)"), bank[2][:]).then_inc(set_dve, 1)
                dve.wait_ge(set_act, 1)
                nc.vector.tensor_scalar(wo_g[:], wo[:], tg[:, 0:1], None, ALU.mult).then_inc(set_dve, 1)

            def set_up_products():
                dve.wait_ge(set_pe, 4)
                nc.vector.tensor_scalar(c_rep[:], ps_s[0][:, 128:256], tg[:, 0:1], None, ALU.mult).then_inc(set_dve, 1)
                for n in range(2):
                    dve.wait_ge(set_pe, 5 + n)
                    nc.vector.tensor_scalar(mix_h[:, n:EXPERTS:2, :], bank[1 + n][:].rearrange("p (e d) -> p e d", d=D),
                                            tg[:, 1:2], None, ALU.mult).then_inc(set_dve, 1)

            def layer_norm(stats_sem, stats, mean_var, norm, src, turn, c):
                for t in range(TILES):
                    last = nc.vector.bn_stats(stats[:, t, :], src[:, t, :])
                last.then_inc(stats_sem, 1)
                wait_chunk(dve, stats_sem, 4, turn, c, 1)
                dve.sem_inc(dve_waited, 1)
                for t in range(TILES):
                    last = nc.vector.bn_aggr(mean_var[:, t, :], stats[:, t, :])
                last.then_inc(stats_sem, 1)
                wait_chunk(dve, stats_sem, 4, turn, c, 2)
                nc.vector.tensor_scalar(norm[:, 1, :], mean_var[:, :, 1], EPS, None, ALU.add).then_inc(stats_sem, 1)
                nc.vector.tensor_scalar(norm[:, 0, :], mean_var[:, :, 0], -1.0, None, ALU.mult).then_inc(stats_sem, 1)

            def rest_of(p, rest, src, col, high, taken, low, turn, b):
                wait_chunk(dve, high, 1, turn, b, 1)
                wait_chunk(dve, low, 1, turn, b - 1, 1)
                nc.vector.scalar_tensor_tensor(rest[:], src[:], bias[:, col:col + 1], p[:, 0, :],
                                               ALU.add, ALU.subtract).then_inc(taken, 1)

            def row_max(turn, i, fill):
                wait_chunk(dve, s_filled, PAIRS, turn, i, fill + 1)
                t, half = fill // 2, fill % 2
                nc.vector.tensor_reduce(nmax[:, :, 4 * half:4 * half + 4, t].rearrange("p g a -> p a g"),
                                        ps_s[fill % 2][:].rearrange("p (a g k) -> p a g k", g=2, k=SEQ),
                                        AX_X, ALU.max, negate=True).then_inc(s_max, 1)

            def normalise(turn, q, half):
                wait_chunk(dve, otr_filled, 2, turn, q, half + 1)
                blocks = bank[1 + half][:].rearrange("p (m w) -> p m w", w=16)
                nc.vector.reciprocal(rden[:, half, :], blocks[:, :, DH]).then_inc(rden_ready, 1)
                wait_chunk(dve, rden_ready, 2, turn, q, half + 1)
                wait_chunk(dve, oT_filled, 1, turn, q - 1, 1)
                nc.vector.tensor_tensor(o_tok[:, :, 64 * half:64 * half + 64].rearrange("p t (m d) -> p t m d", d=DH),
                                        blocks[:, :, 0:DH].rearrange("p (t m) d -> p t m d", t=TILES),
                                        rden[:, half, :].rearrange("p (t m o) -> p t m o", t=TILES, o=1).to_broadcast([P, TILES, 8, DH]),
                                        ALU.mult).then_inc(o_normed, 1)

            def top_two(turn, f):
                wait_chunk(dve, logit_filled, 1, turn, f, 1)
                nc.vector.tensor_copy(logit[:], bank[2][0:CB, 0:EXPERTS]).then_inc(gate_steps, 1)
                wait_chunk(dve, gate_steps, 8, turn, f, 1)
                dve.sem_inc(dve_waited, 1)
                nc.vector.max(top[:], logit[:]).then_inc(gate_steps, 1)
                wait_chunk(dve, gate_steps, 8, turn, f, 2)
                nc.vector.tensor_tensor(gw[:, 0:1], top[:, 1:2], top[:, 0:1], ALU.subtract).then_inc(gate_diff, 1)
                nc.vector.max_index(top_i[:], top[:], logit[:]).then_inc(gate_steps, 1)
                wait_chunk(dve, gate_steps, 8, turn, f, 3)
                nc.vector.tensor_copy(top_f[:], top_i[:]).then_inc(gate_steps, 1)

            def gate(turn, f):
                wait_chunk(dve, gate_exp, 1, turn, f, 1)
                nc.vector.tensor_scalar(gw[:, 2:3], gw[:, 1:2], 1.0, None, ALU.add).then_inc(gate_steps, 1)
                wait_chunk(dve, gate_steps, 8, turn, f, 5)
                nc.vector.reciprocal(gw[:, 3:4], gw[:, 2:3]).then_inc(gate_steps, 1)
                wait_chunk(dve, gate_steps, 8, turn, f, 6)
                nc.vector.tensor_tensor(gw[:, 4:5], gw[:, 1:2], gw[:, 3:4], ALU.mult).then_inc(gate_steps, 1)
                wait_chunk(dve, gate_steps, 8, turn, f, 7)
                nc.vector.tensor_scalar(gate_a[:], col_of[:], top_f[:, 0:1], gw[:, 3:4], ALU.is_equal, ALU.mult)
                nc.vector.tensor_scalar(gate_b[:], col_of[:], top_f[:, 1:2], gw[:, 4:5], ALU.is_equal, ALU.mult).then_inc(gate_steps, 1)
                wait_chunk(dve, gate_steps, 8, turn, f, 8)
                wait_chunk(dve, grep_filled, 1, turn, f - 1, 1)
                nc.vector.tensor_tensor(gates[:], gate_a[:, None, :].to_broadcast([CB, 16, EXPERTS]),
                                        gate_b[:, None, :].to_broadcast([CB, 16, EXPERTS]), ALU.add).then_inc(gates_ready, 1)

            def step(turn, i):
                a, b, q, f = i + 3, i + 2, i - 1, i - 2
                def statistics():
                    wait_half(dve, x_in, 16, turn, a)
                    wait_chunk(dve, xn_ready, TILES, turn, a - 1, TILES)
                    layer_norm(ln1_steps, stats1, mean_var1, norm1, xt[a % 2], turn, a)
                if i == -3:
                    clear_vb(0)
                    statistics()
                    order_qk()
                    clear_vb(1)
                if i == -2:
                    statistics()
                if has(i):
                    row_max(turn, i, 0)
                    row_max(turn, i, 1)
                if has(i):
                    row_max(turn, i, 2)
                    row_max(turn, i, 3)
                    row_max(turn, i, 4)
                    row_max(turn, i, 5)
                if has(f):
                    top_two(turn, f)
                    gate(turn, f)
                if has(i):
                    row_max(turn, i, 6)
                    row_max(turn, i, 7)
                    wait_chunk(dve, s_max, PAIRS, turn, i, PAIRS)
                    wait_chunk(dve, shiftT_filled, 1, turn, i - 1, 1)
                    flat = nmax[:].rearrange("p g a t -> p g (a t)")
                    nc.vector.tensor_copy(shift[:, :, 0, :], flat).then_inc(shift_hi, 1)
                    wait_chunk(dve, shift_hi, 1, turn, i, 1)
                    nc.vector.tensor_tensor(shift[:, :, 1, :], flat, shift[:, :, 0, :], ALU.subtract).then_inc(shift_ready, 1)
                if has(f):
                    if f == 0:
                        dve.wait_ge(consts, 12)
                    wait_chunk(dve, grep_filled, 1, turn, f, 1)
                    wait_chunk(dve, wmix_filled, 2, turn, f - 1, 2)
                    nc.vector.tensor_tensor(gmix[:], bank[2][:, 0:CB].rearrange("p (b o) -> p b o", o=1).to_broadcast([P, CB, 16]),
                                            h16_mask[:, None, :].to_broadcast([P, CB, 16]), ALU.mult).then_inc(gmix_ready, 1)
                if has(q):
                    normalise(turn, q, 0)
                if has(b):
                    rest_of(qp[b % 2], q_rest, ps_t[0], 0, q_high, q_taken, q_parts, turn, b)
                if has(q):
                    normalise(turn, q, 1)
                if has(b):
                    rest_of(kp[b % 2], k_rest, ps_t[1], 1, k_high, k_taken, k_parts, turn, b)
                if has(a) and i > -2:
                    statistics()
                if i == -2:
                    set_up()
                if i == -1:
                    set_up_products()
                if has(f):
                    wait_chunk(dve, y2_filled, 1, turn, f, 1)
                    wait_chunk(dve, x1_scaled, TILES, turn, f, TILES)
                    flat = x1[f % 2][:].rearrange("p t d -> p (t d)")
                    nc.vector.tensor_tensor(flat, bank[2][:], flat, ALU.add).then_inc(out_ready, 1)
                if has(q):
                    wait_chunk(dve, y_filled, 1, turn, q, 1)
                    wait_chunk(dve, xr_ready, 1, turn, q, 1)
                    wait_half(dve, out_done, 16, turn, q - 2)
                    nc.vector.tensor_tensor(x1[q % 2][:].rearrange("p t d -> p (t d)"), bank[1][:],
                                            xr[q % 2][:].rearrange("p t d -> p (t d)"), ALU.add).then_inc(x1_ready, 1)
                    wait_chunk(dve, x1_ready, 1, turn, q, 1)
                    wait_chunk(dve, x1_scaled, TILES, turn, q - 1, TILES)
                    layer_norm(ln2_steps, stats2, mean_var2, norm2, x1[q % 2], turn, q)

            steps(dve, step)

        @block.tensor
        def _(pe):
            mm = nc.tensor.matmul

            def tiles_T(dst, src):
                for t in range(TILES):
                    last = nc.tensor.transpose(dst[:, P * t:P * t + P], src[:, t, :], ident[:])
                return last

            pe.wait_ge(consts, 12)
            pe.wait_ge(qk_cols, 1)
            for n in range(2):
                last = mm(bank[0][:, n:n + 1], b_rowp[:, n, :], ones_f[:, 0:1], start=True, stop=True)
            last.then_inc(bias_filled, 1)

            def set_up():
                pe.wait_ge(w_in, 16 * 9)
                mm(ps_s[0][:, 0:2], ones_f[:], g_row[:], start=True, stop=True).then_inc(set_pe, 1)
                nc.tensor.transpose(ps_s[1][:, 0:EXPERTS], wr_in[:], ident[0:EXPERTS, 0:EXPERTS]).then_inc(set_pe, 1)
                for e4 in range(EXPERTS // 2):
                    last = nc.tensor.transpose(bank[2][:, D * e4:D * e4 + D], bw_in[:, e4, :], ident[:])
                last.then_inc(set_pe, 1)

            def set_up_products():
                pe.wait_ge(set_dve, 3)
                pe.wait_ge(set_act, 1)
                mm(ps_s[0][:, 128:256], bv_rep[:], wo[:], start=True, stop=False)
                mm(ps_s[0][:, 128:256], ones_f[:], bo_row[:], start=False, stop=True).then_inc(set_pe, 1)
                for e in range(EXPERTS):
                    e4, rows = e // 2, slice(RANK * (e % 2), RANK * (e % 2) + RANK)
                    last = mm(bank[1 + e % 2][:, D * e4:D * e4 + D], bwT[rows, e4, :], a_in[rows, e4, :], start=True, stop=True)
                    if e4 == 3:
                        last.then_inc(set_pe, 1)

            def key_scores(turn, q, pair):
                if pair == 0:
                    wait_half(pe, shift_in, 16, turn, q)
                    if q < 2:
                        pe.wait_ge(kb_ones[q], 32)
                if pair >= 2:
                    wait_chunk(pe, t_exp, PAIRS, turn, q, pair - 1)
                elif q < CHUNKS - 2:
                    wait_chunk(pe, (q_taken, k_taken)[pair], 1, turn, q + 2, 1)
                else:
                    wait_chunk(pe, t_exp, PAIRS, turn, q - 1, PAIRS - 1 + pair)
                n = q % 2
                for b in range(CB):
                    cols = slice(SEQ * b, SEQ * b + SEQ)
                    last = mm(ps_t[pair % 2][:, cols], kb[n][0:ROWS + SHIFT, pair, b, :, :], qa[n][0:ROWS + SHIFT, pair, cols],
                              start=True, stop=True)
                last.then_inc(t_filled, 1)

            def query_scores(turn, i, fill):
                if fill < 2 and i >= 3:
                    wait_chunk(pe, wmix_taken, 2, turn, i - 3, fill + 1)
                else:
                    wait_chunk(pe, s_max, PAIRS, turn, i - (fill < 2), (fill - 2) % PAIRS + 1)
                n, t = i % 2, fill // 2
                for a in range(4):
                    pair = 4 * (fill % 2) + a
                    for b2 in range(2):
                        cols = slice(P * t + SEQ * b2, P * t + SEQ * b2 + SEQ)
                        last = mm(ps_s[fill % 2][SEQ * b2:SEQ * b2 + SEQ, P * a:P * a + P], qa[n][0:ROWS, pair, cols],
                                  kb[n][0:ROWS, pair, 2 * t + b2, :, :], start=True, stop=True)
                last.then_inc(s_filled, 1)

            def times_v(turn, q, half, batches):
                if batches[0] == 0:
                    wait_chunk(pe, t_exp, PAIRS, turn, q, 4 * half + 4)
                    wait_chunk(pe, o_taken, 2, turn, q - (half == 0), 2 - half)
                    if half == 0:
                        wait_chunk(pe, v_taken, 2, turn, q, 2)
                for b in batches:
                    cols = slice(SEQ * b, SEQ * b + SEQ)
                    for a in range(4):
                        last = mm(ps_o[VW * a:VW * a + VW, cols], vb[q % 2][:, b, 4 * half + a, :], prob[:, 4 * half + a, cols],
                                  start=True, stop=True, tile_position=(0, VW * a))
                return last

            def o_back(turn, q, half):
                wait_chunk(pe, o_taken, 2, turn, q, half + 1)
                if half == 0:
                    wait_chunk(pe, x1_ready, 1, turn, q - 1, 1)
                elif q < CHUNKS - 1:
                    wait_chunk(pe, shiftT_taken, 1, turn, q + 1, 1)
                else:
                    wait_chunk(pe, gmix_ready, 1, turn, q - 1, 1)
                for t in range(TILES):
                    last = nc.tensor.transpose(bank[1 + half][:, P * t:P * t + P], oaug[:, half, P * t:P * t + P], ident[:])
                last.then_inc(otr_filled, 1)

            def mix_half(turn, f, n):
                if f < CHUNKS - 2:
                    wait_chunk(pe, s_max, PAIRS, turn, f + 2, PAIRS - 1 + n)
                else:
                    wait_chunk(pe, wmix_taken, 2, turn, f - 1, n + 1)
                for hc in range(4):
                    last = mm(ps_s[n][:, P * hc:P * hc + P], mix[:, 4 * n + hc, :], gmix[:].rearrange("p b h -> p (b h)"),
                              start=True, stop=True)
                last.then_inc(wmix_filled, 1)

            def step(turn, i):
                b, v, q, f = i + 2, i + 1, i - 1, i - 2

                def values(batches):
                    for bb in batches:
                        for h2 in range(2):
                            last = mm(bank[0][64 * h2:64 * h2 + 64, 64 * bb:64 * bb + 64], cT[v % 2][:, SEQ * bb:SEQ * bb + SEQ],
                                      wv[:].rearrange("p (a g d) -> p g a d", g=2, d=DH)[:, h2], start=True, stop=True)
                    return last

                def shift_rows():
                    wait_chunk(pe, shift_ready, 1, turn, i, 1)
                    if has(f):
                        wait_chunk(pe, gmix_ready, 1, turn, f, 1)
                    else:
                        wait_chunk(pe, shiftT_taken, 1, turn, i - 1, 1)
                    nc.tensor.transpose(bank[2][:, 0:64].bitcast(BF16), shift[:].rearrange("p g h m -> p (g h m)"), identb[:]).then_inc(shiftT_filled, 1)

                if has(q):
                    key_scores(turn, q, 0)
                    key_scores(turn, q, 1)
                if has(v):
                    wait_chunk(pe, cT_taken, 1, turn, v, 1)
                    if v == 0:
                        pe.wait_ge(bias_ready, 1)
                        pe.wait_ge(w_in, 16 * 9)
                    if v >= 3:
                        wait_chunk(pe, oT_taken, 1, turn, v - 3, 1)
                    else:
                        wait_chunk(pe, v_taken, 2, turn, v - 1, 2)
                    values(range(CB // 2))
                if has(q):
                    key_scores(turn, q, 2)
                if has(v):
                    values(range(CB // 2, CB)).then_inc(v_filled, 1)
                if has(q):
                    key_scores(turn, q, 3)
                if has(i):
                    if i == 0:
                        pe.wait_ge(set_dve, 7)
                    wait_half(pe, qa_in, 16 * TERMS, turn, i)
                    wait_half(pe, kb_in, 32 * TERMS, turn, i)
                    query_scores(turn, i, 0)
                if has(q):
                    key_scores(turn, q, 4)
                if has(i):
                    query_scores(turn, i, 1)
                if has(q):
                    key_scores(turn, q, 5)
                if has(q):
                    times_v(turn, q, 0, range(CB // 2))
                    key_scores(turn, q, 6)
                if has(i):
                    query_scores(turn, i, 2)
                if has(q):
                    times_v(turn, q, 0, range(CB // 2, CB)).then_inc(o_filled, 1)
                    key_scores(turn, q, 7)
                if has(i):
                    query_scores(turn, i, 3)
                if has(f):
                    wait_chunk(pe, xn2_ready, TILES, turn, f, TILES)
                    if f >= 1:
                        wait_chunk(pe, out_ready, 1, turn, f - 1, 1)
                    else:
                        wait_chunk(pe, o_normed, 2, turn, f, 2)
                    tiles_T(bank[2], xn2).then_inc(x2T_filled, 1)
                if has(i):
                    query_scores(turn, i, 4)
                    query_scores(turn, i, 5)
                if has(f):
                    wait_chunk(pe, x2T_taken, 1, turn, f, 1)
                    mm(bank[2][0:CB, 0:EXPERTS], x2T[:, 0:TOK:SEQ], wrT[:], start=True, stop=True).then_inc(logit_filled, 1)
                if has(q):
                    times_v(turn, q, 1, range(CB)).then_inc(o_filled, 1)
                if has(i):
                    query_scores(turn, i, 6)
                if i == 0:
                    query_scores(turn, i, 7)
                if has(b):
                    wait_chunk(pe, xn_ready, TILES, turn, b, TILES)
                    if b >= 3:
                        wait_chunk(pe, t_exp, PAIRS, turn, b - 3, PAIRS - 1)
                    else:
                        wait_chunk(pe, q_taken, 1, turn, b - 1, 1)
                    tiles_T(ps_t[0], xn).then_inc(xnT_filled, 1)
                    wait_half(pe, c_in, 16, turn, b)
                    if b >= 3:
                        wait_chunk(pe, t_exp, PAIRS, turn, b - 3, PAIRS)
                    else:
                        wait_chunk(pe, k_taken, 1, turn, b - 1, 1)
                    tiles_T(ps_t[1], ct[b % 2]).then_inc(cT_filled, 1)
                if has(i) and i > 0:
                    query_scores(turn, i, 7)
                if i == 0:
                    shift_rows()
                if has(q):
                    o_back(turn, q, 0)
                if has(b):
                    if b == 0:
                        pe.wait_ge(qk_cols, 3)
                    wait_chunk(pe, xnT_taken, 1, turn, b, 1)
                    mm(ps_t[0][:], wq_p[:], xnT[:], start=True, stop=True).then_inc(q_filled, 1)
                if has(f):
                    wait_chunk(pe, gates_ready, 1, turn, f, 1)
                    mm(bank[2][:, 0:CB], gates[:].rearrange("b h e -> b (h e)"), ident[0:CB, 0:CB],
                       start=True, stop=True).then_inc(grep_filled, 1)
                if has(b):
                    wait_chunk(pe, cT_taken, 1, turn, b, 1)
                    mm(ps_t[1][:], wk_p[:], cT[b % 2][:], start=True, stop=True).then_inc(k_filled, 1)
                if has(i) and i > 0:
                    shift_rows()
                if has(f):
                    if f == 0:
                        pe.wait_ge(mix_in, 16 * HC)
                    wait_chunk(pe, gmix_ready, 1, turn, f, 1)
                    mix_half(turn, f, 0)
                if has(q):
                    o_back(turn, q, 1)
                if has(f):
                    mix_half(turn, f, 1)
                if has(q):
                    wait_chunk(pe, o_normed, 2, turn, q, 2)
                    if q < CHUNKS - 2:
                        wait_chunk(pe, v_taken, 2, turn, q + 2, 2)
                    else:
                        wait_chunk(pe, oT_taken, 1, turn, q - 1, 1)
                    tiles_T(bank[0], o_tok).then_inc(oT_filled, 1)
                if has(f):
                    wait_chunk(pe, wmix_taken, 2, turn, f, 2)
                    if f < CHUNKS - 1:
                        wait_chunk(pe, o_normed, 2, turn, f + 1, 2)
                    for bb in range(CB):
                        rows = slice(64 * (bb % 2), 64 * (bb % 2) + 64)
                        last = mm(bank[2][rows, D * (bb // 2):D * (bb // 2) + D], x2T[:, SEQ * bb:SEQ * bb + SEQ], wmix[:, bb, :],
                                  start=True, stop=True)
                    last.then_inc(y2_filled, 1)
                if has(q):
                    wait_chunk(pe, oT_taken, 1, turn, q, 1)
                    for t in range(TILES):
                        last = mm(bank[1][:, D * t:D * t + D], oT[:, P * t:P * t + P], wo_g[:], start=True, stop=True)
                    last.then_inc(y_filled, 1)
                if i == -2:
                    set_up()
                if i == -1:
                    set_up_products()

            steps(pe, step)


_INS = ['x', 'ctx_1024', 'g_xattn', 'g_ffn', 'L0_xattn_Wq', 'L0_xattn_bq', 'L0_xattn_Wk', 'L0_xattn_bk', 'L0_xattn_Wv',
        'L0_xattn_bv', 'L0_xattn_Wo', 'L0_xattn_bo', 'L0_ffn_Wr', 'L0_ffn_A', 'L0_ffn_Bw']


def kernel(**inputs):
    import numpy as _np
    import concourse.bacc as _bacc
    from concourse import mybir as _mybir
    from concourse.bass_utils import run_bass_kernel_spmd as _run

    nc = _bacc.Bacc("TRN2", target_bir_lowering=False, num_devices=1)
    arrays, args = {}, []
    for name in _INS:
        a = _np.ascontiguousarray(inputs[name])
        arrays[f"in_{name}_dram"] = a
        args.append(nc.dram_tensor(f"in_{name}_dram", a.shape, _mybir.dt.from_np(a.dtype), kind="ExternalInput").ap())
    args.append(nc.dram_tensor("out_0_dram", (BATCHES, SEQ, D), _mybir.dt.float32, kind="ExternalOutput").ap())
    block_attention_experts(nc, *args)
    r = _run(nc, [arrays], core_ids=[0])
    return r.results[0]["out_0_dram"]
```

```python
from contextlib import ExitStack

import concourse.bass as bass
from concourse import mybir

P = 128
BATCHES, SEQ, D = 128, 64, 128
HEADS, DH = 16, 8
PAIRS = HEADS // 2
EXPERTS, RANK = 8, 64
CB = 8
CHUNKS = BATCHES // CB
TOK = CB * SEQ
TILES = TOK // P
Q_PART = (0, 1, 2, 0, 1, 0)
K_PART = (0, 0, 0, 1, 1, 2)
TERMS = len(Q_PART)
ROWS = TERMS * 2 * DH
SHIFT = 4
VW = 32
HC = D // 16
EPS = 1e-5

ALU = mybir.AluOpType
ACT = mybir.ActivationFunctionType
BF16 = mybir.dt.bfloat16
F32 = mybir.dt.float32
U32 = mybir.dt.uint32
AX_X = mybir.AxisListType.X

FIRST, LAST = -4, CHUNKS + 1
LOOP_FIRST = 3
LOOP_TURNS = (CHUNKS - 4 - LOOP_FIRST) // 2
LOOP_END = LOOP_FIRST + 2 * LOOP_TURNS


def block_attention_experts(nc, x, ctx_in, g_xattn, g_ffn, Wq, bq, Wk, bk, Wv, bv, Wo, bo, Wr, A, Bw, out):
    x_v = x.rearrange("(c t b) s d -> c (b s) t d", t=TILES, b=2)
    c_v = ctx_in.rearrange("(c t b) s d -> c (b s) t d", t=TILES, b=2)
    o_v = out.rearrange("(c t b) s d -> c (b s) t d", t=TILES, b=2)

    stack = ExitStack()
    with stack:
        def sb(name, shape, dt=F32):
            return stack.enter_context(nc.sbuf_tensor(name, shape, dt))

        def pb(name, shape, dt=F32):
            return stack.enter_context(nc.psum_tensor(name, shape, dt))

        def sem(name):
            return stack.enter_context(nc.semaphore(name))

        def two(make, name, shape, dt=F32):
            return [make(f"{name}{n}", shape, dt) for n in range(2)]

        ident = sb("ident", [P, P])
        identb = sb("identb", [P, P], BF16)
        ones_f = sb("ones_f", [1, P])
        one_f = sb("one_f", [P, 1])
        minus_half = sb("minus_half", [P, TILES])
        ones_b = sb("ones_b", [2 * PAIRS, TOK], BF16)
        col_of = sb("col_of", [CB, EXPERTS])
        h16_mask = sb("h16_mask", [P, 16])
        wq, wk, wv, wo, wo_g = (sb(n, [P, D]) for n in ("wq", "wk", "wv", "wo", "wo_g"))
        wq_p, wk_p = sb("wq_p", [P, D]), sb("wk_p", [P, D])
        b_row = sb("b_row", [1, 2, D])
        b_rowp = sb("b_rowp", [1, 2, D])
        bias = sb("bias", [P, 2])
        bv_col = sb("bv_col", [P, 1])
        bo_row = sb("bo_row", [1, D])
        bv_rep = sb("bv_rep", [P, P])
        g_row = sb("g_row", [1, 2])
        tg = sb("tg", [P, 2])
        c_rep = sb("c_rep", [P, D])
        wr_in = sb("wr_in", [EXPERTS, D])
        wrT = sb("wrT", [D, EXPERTS])
        a_in = sb("a_in", [P, EXPERTS // 2, D])
        bw_in = sb("bw_in", [D, EXPERTS // 2, P])
        bwT = sb("bwT", [P, EXPERTS // 2, D])
        mix_h = sb("mix_h", [P, EXPERTS, D])
        mix = sb("mix", [P, HC, D])

        xt = two(sb, "xt", [P, TILES, D])
        ct = two(sb, "ct", [P, TILES, D])
        stats1 = sb("stats1", [P, TILES, 6])
        mean_var1 = sb("mean_var1", [P, TILES, 2])
        norm1 = sb("norm1", [P, 4, TILES])
        stats2 = sb("stats2", [P, TILES, 6])
        mean_var2 = sb("mean_var2", [P, TILES, 2])
        norm2 = sb("norm2", [P, 6, TILES])
        xn = sb("xn", [P, TILES, D])
        xnT = sb("xnT", [D, TOK])
        cT = two(sb, "cT", [D, TOK])
        qp = two(sb, "qp", [P, 3, TOK], BF16)
        kp = two(sb, "kp", [P, 3, TOK], BF16)
        q_rest = sb("q_rest", [P, TOK])
        k_rest = sb("k_rest", [P, TOK])
        qa = two(sb, "qa", [P, PAIRS, TOK], BF16)
        kb = two(sb, "kb", [P, PAIRS, CB, 2, SEQ], BF16)
        vb = two(sb, "vb", [P, CB, PAIRS, VW])
        nmax = sb("nmax", [P, 2, PAIRS, TILES])
        shift = sb("shift", [P, 2, 2, PAIRS * TILES], BF16)
        shiftT = sb("shiftT", [P, P], BF16)
        prob = sb("prob", [P, PAIRS, TOK])
        oaug = sb("oaug", [P, 2, TOK])
        rden = sb("rden", [P, 2, 32])
        o_tok = sb("o_tok", [P, TILES, D])
        oT = sb("oT", [D, TOK])
        xr = two(sb, "xr", [P, TILES, D])
        x1 = two(sb, "x1", [P, TILES, D])
        xn2 = sb("xn2", [P, TILES, D])
        x2T = sb("x2T", [D, TOK])
        logit = sb("logit", [CB, EXPERTS])
        top = sb("top", [CB, EXPERTS])
        top_i = sb("top_i", [CB, EXPERTS], U32)
        top_f = sb("top_f", [CB, EXPERTS])
        gw = sb("gw", [CB, 6])
        gate_a = sb("gate_a", [CB, EXPERTS])
        gate_b = sb("gate_b", [CB, EXPERTS])
        gates = sb("gates", [CB, 16, EXPERTS])
        gmix = sb("gmix", [P, CB, 16])
        wmix = sb("wmix", [D, CB, D])

        ps_s = two(pb, "ps_s", [P, TOK])
        ps_t = two(pb, "ps_t", [P, TOK])
        ps_o = pb("ps_o", [P, TOK])
        bank = [pb(f"bank{n}", [P, TOK]) for n in range(3)]

        w_qk_in, w_in = sem("w_qk_in"), sem("w_in")
        pool_waited, dve_waited, sp_waited = sem("pool_waited"), sem("dve_waited"), sem("sp_waited")
        mix_in = sem("mix_in")
        kb_ones = [sem(f"kb_ones{n}") for n in range(2)]
        consts, ones_ready = sem("consts"), sem("ones_ready")
        qk_cols, bias_filled, bias_ready = sem("qk_cols"), sem("bias_filled"), sem("bias_ready")
        kb_cleared, vb_cleared, vb_ones = sem("kb_cleared"), sem("vb_cleared"), sem("vb_ones")
        set_pe = sem("set_pe")
        set_dve = sem("set_dve")
        set_act = sem("set_act")
        x_in = [sem(f"x_in{n}") for n in range(2)]
        c_in = [sem(f"c_in{n}") for n in range(2)]
        xr_in = [sem(f"xr_in{n}") for n in range(2)]
        qa_in = [sem(f"qa_in{n}") for n in range(2)]
        kb_in = [sem(f"kb_in{n}") for n in range(2)]
        shift_in = [sem(f"shift_in{n}") for n in range(2)]
        out_done = [sem(f"out_done{n}") for n in range(2)]
        ln1_steps = sem("ln1_steps")
        ln2_steps = sem("ln2_steps")
        rstd1_ready, rstd2_ready = sem("rstd1_ready"), sem("rstd2_ready")
        xn_ready = sem("xn_ready")
        xnT_filled, xnT_taken = sem("xnT_filled"), sem("xnT_taken")
        cT_filled, cT_taken = sem("cT_filled"), sem("cT_taken")
        q_filled, q_high, q_taken, q_mid, q_parts = (sem(n) for n in ("q_filled", "q_high", "q_taken", "q_mid", "q_parts"))
        k_filled, k_high, k_taken, k_mid, k_parts = (sem(n) for n in ("k_filled", "k_high", "k_taken", "k_mid", "k_parts"))
        v_filled, v_taken = sem("v_filled"), sem("v_taken")
        s_filled, s_max = sem("s_filled"), sem("s_max")
        shift_hi, shift_ready = sem("shift_hi"), sem("shift_ready")
        shiftT_filled, shiftT_taken = sem("shiftT_filled"), sem("shiftT_taken")
        t_filled, t_exp = sem("t_filled"), sem("t_exp")
        o_filled, o_taken = sem("o_filled"), sem("o_taken")
        otr_filled, rden_ready, o_normed = sem("otr_filled"), sem("rden_ready"), sem("o_normed")
        oT_filled, oT_taken = sem("oT_filled"), sem("oT_taken")
        xr_ready = sem("xr_ready")
        y_filled, x1_ready = sem("y_filled"), sem("x1_ready")
        xn2_ready, x1_scaled = sem("xn2_ready"), sem("x1_scaled")
        x2T_filled, x2T_taken = sem("x2T_filled"), sem("x2T_taken")
        logit_filled, gate_steps, gate_diff, gate_exp, gates_ready = (
            sem(n) for n in ("logit_filled", "gate_steps", "gate_diff", "gate_exp", "gates_ready"))
        grep_filled, gmix_ready = sem("grep_filled"), sem("gmix_ready")
        wmix_filled, wmix_taken = sem("wmix_filled"), sem("wmix_taken")
        y2_filled, out_ready = sem("y2_filled"), sem("out_ready")

        block = stack.enter_context(nc.Block())

        def steps(eng, step):
            for i in range(FIRST, LOOP_FIRST):
                step(0, i)
            with eng.Fori(0, LOOP_TURNS) as turn:
                step(turn, LOOP_FIRST)
                step(turn, LOOP_FIRST + 1)
            for i in range(LOOP_END, LAST + 1):
                step(0, i)

        def has(c):
            return 0 <= c < CHUNKS

        def wait_chunk(eng, s, per, turn, c, n):
            if per * c + n > 0 and c >= 0:
                eng.wait_ge(s, 2 * per * turn + (per * c + n))

        def back_bank(q, half):
            return bank[1] if half == 0 else bank[2] if q < CHUNKS - 1 else ps_t[0]

        def wait_half(eng, pair_of_sems, per, turn, c):
            if c >= 0:
                eng.wait_ge(pair_of_sems[c % 2], per * turn + per * (c // 2 + 1))

        @block.sync
        def _(sp):
            def load_qk_weights():
                for dst, src in ((wq[:], Wq), (b_row[:, 0, :], bq.rearrange("(o n) -> o n", o=1)),
                                 (b_row[:, 1, :], bk.rearrange("(o n) -> o n", o=1)), (wk[:], Wk)):
                    sp.dma_start(dst, src).then_inc(w_qk_in, 16)

            def load_weights():
                for dst, src in ((wv[:], Wv), (wo[:], Wo),
                                 (bv_col[:], bv.rearrange("(p o) -> p o", o=1)),
                                 (bo_row[:], bo.rearrange("(o n) -> o n", o=1)),
                                 (g_row[:, 0:1], g_xattn.rearrange("(o n) -> o n", o=1)),
                                 (g_row[:, 1:2], g_ffn.rearrange("(o n) -> o n", o=1)),
                                 (wr_in[:], Wr),
                                 (a_in[:], A.rearrange("(e4 e2) r d -> (e2 r) e4 d", e2=2)),
                                 (bw_in[:].rearrange("h e4 (e2 r) -> h (e4 e2) r", e2=2), Bw.rearrange("e h r -> h e r"))):
                    sp.dma_start(dst, src).then_inc(w_in, 16)

            def lay_ones(n):
                sp.wait_ge(ones_ready, 1)
                sp.wait_ge(kb_cleared, n + 1)
                for h2 in range(2):
                    row = ROWS + 2 * h2
                    sp.dma_start(kb[n][row:row + 2, :, :, h2, :], ones_b[:, :]).then_inc(kb_ones[n], 16)

            def spread_mix():
                sp.wait_ge(set_dve, 7)
                for hc in range(HC):
                    sp.dma_start(mix[:, hc, :], mix_h[16 * hc:16 * hc + 16, :, :]).then_inc(mix_in, 16)

            def step(turn, i):
                l, v, f = i + 4, i + 1, i - 2

                def load_x():
                    source = x_v[bass.ds(2 * turn + l, 1)].rearrange("o p t d -> p (o t) d")
                    wait_chunk(sp, xn_ready, TILES, turn, l - 2, TILES)
                    sp.dma_start(xt[l % 2][:], source).then_inc(x_in[l % 2], 16)

                if l in (0, 1):
                    load_x()
                    sp.dma_start(ct[l][:], c_v[bass.ds(l, 1)].rearrange("o p t d -> p (o t) d")).then_inc(c_in[l], 16)
                if l == 0:
                    load_qk_weights()
                if l == 1:
                    load_weights()
                if has(i):
                    wait_chunk(sp, x1_ready, 1, turn, i - 2, 1)
                    source = x_v[bass.ds(2 * turn + i, 1)].rearrange("o p t d -> p (o t) d")
                    sp.dma_start(xr[i % 2][:], source).then_inc(xr_in[i % 2], 16)
                if has(v):
                    n = v % 2
                    if v < 2:
                        lay_ones(v)
                    if v >= 2:
                        wait_chunk(sp, t_filled, PAIRS, turn, v - 2, PAIRS)
                        sp.sem_inc(sp_waited, 1)
                    for part, q_ready, k_ready in ((0, q_high, k_high), (1, q_mid, k_mid), (2, q_parts, k_parts)):
                        wait_chunk(sp, q_ready, 1, turn, v, 1)
                        for t in range(TERMS):
                            if Q_PART[t] == part:
                                sp.dma_start(qa[n][16 * t:16 * t + 16, :, :], qp[n][:, part, :]).then_inc(qa_in[n], 16)
                        wait_chunk(sp, k_ready, 1, turn, v, 1)
                        for t in range(TERMS):
                            for h2 in range(2):
                                if K_PART[t] == part:
                                    r = 16 * t + 8 * h2
                                    sp.dma_start(kb[n][r:r + DH, :, :, h2, :], kp[n][64 * h2:64 * h2 + 64, part, :]).then_inc(kb_in[n], 16)
                if has(l) and l >= 2:
                    load_x()
                if i == 0:
                    spread_mix()
                if has(l) and l >= 2:
                    source = c_v[bass.ds(2 * turn + l, 1)].rearrange("o p t d -> p (o t) d")
                    wait_chunk(sp, cT_filled, 1, turn, l - 2, 1)
                    sp.dma_start(ct[l % 2][:], source).then_inc(c_in[l % 2], 16)
                if has(f):
                    wait_chunk(sp, out_ready, 1, turn, f, 1)
                    target = o_v[bass.ds(2 * turn + f, 1)].rearrange("o p t d -> p (o t) d")
                    sp.dma_start(target, x1[f % 2][:]).then_inc(out_done[f % 2], 16)

            steps(sp, step)
            for n in range(2):
                sp.wait_ge(out_done[n], 16 * CHUNKS // 2)

        @block.gpsimd
        def _(pool):
            pool.memset(ident[:], 0.0).then_inc(consts, 1)
            pool.memset(identb[:], 0.0).then_inc(consts, 1)
            pool.memset(h16_mask[:], 1.0).then_inc(consts, 1)
            pool.memset(ones_b[:], 1.0).then_inc(ones_ready, 1)
            pool.memset(minus_half[:], -0.5).then_inc(consts, 1)
            pool.memset(ones_f[:], 1.0).then_inc(consts, 1)
            pool.memset(one_f[:], 1.0).then_inc(consts, 1)
            pool.iota(top_i[:], [[1, EXPERTS]], base=0, channel_multiplier=0).then_inc(consts, 1)
            pool.wait_ge(consts, 7)
            pool.tensor_copy(col_of[:], top_i[:]).then_inc(consts, 1)
            for m in (ident, identb):
                pool.affine_select(out=m[:], in_=m[:], compare_op=ALU.not_equal, fill=1.0,
                                   base=0, pattern=[[-1, P]], channel_multiplier=1).then_inc(consts, 1)
            pool.affine_select(out=h16_mask[:], in_=h16_mask[:], compare_op=ALU.is_ge, fill=0.0,
                               base=0, pattern=[[-8, 16]], channel_multiplier=1).then_inc(consts, 1)
            pool.wait_ge(consts, 11)
            pool.affine_select(out=h16_mask[:], in_=h16_mask[:], compare_op=ALU.is_ge, fill=0.0,
                               base=7, pattern=[[8, 16]], channel_multiplier=-1).then_inc(consts, 1)

            def clear_kb(n):
                pool.memset(kb[n][:].rearrange("p a b g k -> p (a b g k)").bitcast(F32), 0.0).then_inc(kb_cleared, 1)

            def rstd(stats_sem, norm, done, n, turn, c):
                wait_chunk(pool, stats_sem, 4, turn, c, 4)
                pool.tensor_tensor(norm[:, 2, :], norm[:, 1, :], minus_half[:], ALU.pow).then_inc(done, 1)
                wait_chunk(pool, done, n, turn, c, 1)
                pool.tensor_tensor(norm[:, 3, :], norm[:, 0, :], norm[:, 2, :], ALU.mult).then_inc(done, 1)

            def low_part(ready, p, rest, done, turn, b):
                wait_chunk(pool, ready, 1, turn, b, 1)
                pool.tensor_tensor(p[:, 2, :], rest[:], p[:, 1, :], ALU.subtract).then_inc(done, 1)

            def step(turn, i):
                b, q, f = i + 2, i - 1, i - 2

                def rstd_in():
                    rstd(ln1_steps, norm1, rstd1_ready, 2, turn, b)

                def rstd_x1():
                    rstd(ln2_steps, norm2, rstd2_ready, 4, turn, f)

                def normalise_x1():
                    wait_chunk(pool, rstd2_ready, 4, turn, f, 2)
                    wait_chunk(pool, x2T_filled, 1, turn, f - 1, 1)
                    pool.sem_inc(pool_waited, 1)
                    for t in range(TILES):
                        pool.tensor_scalar(xn2[:, t, :], x1[f % 2][:, t, :], norm2[:, 2, t:t + 1], norm2[:, 3, t:t + 1],
                                           ALU.mult, ALU.add).then_inc(xn2_ready, 1)

                def normalise_in():
                    wait_chunk(pool, rstd1_ready, 2, turn, b, 2)
                    wait_chunk(pool, xnT_filled, 1, turn, b - 1, 1)
                    wait_half(pool, x_in, 16, turn, b)
                    pool.sem_inc(pool_waited, 1)
                    for t in range(TILES):
                        pool.tensor_scalar(xn[:, t, :], xt[b % 2][:, t, :], norm1[:, 2, t:t + 1], norm1[:, 3, t:t + 1],
                                           ALU.mult, ALU.add).then_inc(xn_ready, 1)

                def add_constant():
                    if q == 0:
                        pool.wait_ge(set_dve, 5)
                    wait_half(pool, xr_in, 16, turn, q)
                    pool.tensor_tensor(xr[q % 2][:], xr[q % 2][:], c_rep[:, None, :].to_broadcast([P, TILES, D]),
                                       ALU.add).then_inc(xr_ready, 1)

                def scale_x1():
                    pool.tensor_scalar(norm2[:, 4, :], norm2[:, 2, :], tg[:, 1:2], one_f[:, 0:1], ALU.mult, ALU.add).then_inc(rstd2_ready, 1)
                    pool.tensor_scalar(norm2[:, 5, :], norm2[:, 3, :], tg[:, 1:2], None, ALU.mult).then_inc(rstd2_ready, 1)
                    wait_chunk(pool, rstd2_ready, 4, turn, f, 4)
                    wait_chunk(pool, xn2_ready, TILES, turn, f, TILES)
                    pool.sem_inc(pool_waited, 1)
                    for t in range(TILES):
                        pool.tensor_scalar(x1[f % 2][:, t, :], x1[f % 2][:, t, :], norm2[:, 4, t:t + 1], norm2[:, 5, t:t + 1],
                                           ALU.mult, ALU.add).then_inc(x1_scaled, 1)

                def place_shift():
                    wait_chunk(pool, shiftT_taken, 1, turn, i, 1)
                    pool.sem_inc(pool_waited, 1)
                    pool.dma_start(qa[i % 2][ROWS:ROWS + SHIFT, :, :].rearrange("r a n -> r (a n)"), shiftT[:, :]).then_inc(shift_in[i % 2], 16)

                if i in (-2, -1):
                    rstd_in()
                    normalise_in()
                    clear_kb(i + 2)
                    low_part(q_mid, qp[b % 2], q_rest, q_parts, turn, b)
                    low_part(k_mid, kp[b % 2], k_rest, k_parts, turn, b)
                    return
                if has(b):
                    rstd_in()
                if has(f):
                    rstd_x1()
                    normalise_x1()
                if has(b):
                    normalise_in()
                if has(q):
                    add_constant()
                if has(f):
                    scale_x1()
                if has(i):
                    place_shift()
                if has(b):
                    low_part(q_mid, qp[b % 2], q_rest, q_parts, turn, b)
                    low_part(k_mid, kp[b % 2], k_rest, k_parts, turn, b)

            steps(pool, step)

        @block.scalar
        def _(act):
            def copy(dst, src, filled, per, turn, c, n, done):
                wait_chunk(act, filled, per, turn, c, n)
                nc.scalar.activation(dst, src, ACT.Copy).then_inc(done, 1)

            def high_part(p, src, col, filled, high, landed, per, turn, b):
                wait_half(act, landed, per, turn, b - 2)
                wait_chunk(act, filled, 1, turn, b, 1)
                nc.scalar.activation(p[:, 0, :], src[:], ACT.Identity, bias=bias[:, col:col + 1]).then_inc(high, 1)

            def middle_part(p, rest, taken, mid, turn, b):
                wait_chunk(act, taken, 1, turn, b, 1)
                nc.scalar.activation(p[:, 1, :], rest[:], ACT.Copy).then_inc(mid, 1)

            def mixed(turn, f, n):
                copy(wmix[:, :, 64 * n:64 * n + 64].rearrange("p b (c h) -> p b c h", h=16),
                     ps_s[n][:].rearrange("p (c b h) -> p b c h", b=CB, h=16),
                     wmix_filled, 2, turn, f, n + 1, wmix_taken)

            def exp(turn, q, pair):
                wait_chunk(act, t_filled, PAIRS, turn, q, pair + 1)
                wait_chunk(act, o_filled, 2, turn, q - 1, pair // 4 + 1)
                nc.scalar.activation(prob[:, pair, :], ps_t[pair % 2][:], ACT.Exp, scale=DH ** -0.5).then_inc(t_exp, 1)

            def step(turn, i):
                b, v, q, f = i + 2, i + 1, i - 1, i - 2

                def take_x2T():
                    wait_chunk(act, y2_filled, 1, turn, f - 1, 1)
                    copy(x2T[:], bank[2][:], x2T_filled, 1, turn, f, 1, x2T_taken)

                def gate_exponential():
                    wait_chunk(act, gate_diff, 1, turn, f, 1)
                    nc.scalar.activation(gw[:, 1:2], gw[:, 0:1], ACT.Exp).then_inc(gate_exp, 1)

                def take_weighted(half):
                    wait_chunk(act, otr_filled, 2, turn, q - 1, half + 1)
                    copy(oaug[:, half, :], ps_o[:], o_filled, 2, turn, q, half + 1, o_taken)

                def take_xnT():
                    wait_chunk(act, q_filled, 1, turn, b - 1, 1)
                    copy(xnT[:], ps_t[0][:], xnT_filled, 1, turn, b, 1, xnT_taken)

                def take_cT():
                    wait_chunk(act, v_filled, 1, turn, b - 2, 1)
                    copy(cT[b % 2][:], ps_t[1][:], cT_filled, 1, turn, b, 1, cT_taken)

                def q_high_part():
                    if b == 0:
                        act.wait_ge(bias_ready, 1)
                    high_part(qp[b % 2], ps_t[0], 0, q_filled, q_high, qa_in, 16 * TERMS, turn, b)

                def k_high_part():
                    high_part(kp[b % 2], ps_t[1], 1, k_filled, k_high, kb_in, 32 * TERMS, turn, b)

                def take_values(h2):
                    if v == 0 and h2 == 0:
                        act.wait_ge(vb_ones, 4)
                    wait_chunk(act, o_filled, 2, turn, v - 2, 2)
                    copy(vb[v % 2][64 * h2:64 * h2 + 64, :, :, 16 * h2:16 * h2 + DH].rearrange("p b a d -> p (b a) d"),
                         bank[0][64 * h2:64 * h2 + 64, :].rearrange("p (m d) -> p m d", d=DH), v_filled, 1, turn, v, 1, v_taken)

                def shift_rows():
                    wait_half(act, shift_in, 16, turn, i - 1)
                    copy(shiftT[:], bank[2][:, 0:64].bitcast(BF16), shiftT_filled, 1, turn, i, 1, shiftT_taken)

                def take_oT():
                    wait_chunk(act, y_filled, 1, turn, q - 1, 1)
                    copy(oT[:], ps_s[0][:], oT_filled, 1, turn, q, 1, oT_taken)

                if i == 0:
                    take_xnT()
                    take_cT()
                    shift_rows()
                    q_high_part()
                    take_values(0)
                    k_high_part()
                    take_values(1)
                    middle_part(qp[b % 2], q_rest, q_taken, q_mid, turn, b)
                    middle_part(kp[b % 2], k_rest, k_taken, k_mid, turn, b)
                    return
                if i == CHUNKS:
                    for pair in range(PAIRS):
                        exp(turn, q, pair)
                    take_x2T()
                    take_weighted(0)
                    gate_exponential()
                    take_weighted(1)
                    take_oT()
                    mixed(turn, f, 0)
                    mixed(turn, f, 1)
                    return
                if has(q):
                    for pair in range(PAIRS):
                        exp(turn, q, pair)
                    take_weighted(0)
                if has(f):
                    take_x2T()
                    gate_exponential()
                if has(q):
                    take_weighted(1)
                if has(b):
                    take_xnT()
                    take_cT()
                if has(v):
                    take_values(0)
                if has(b):
                    q_high_part()
                if has(i):
                    shift_rows()
                if has(v):
                    take_values(1)
                if has(b):
                    k_high_part()
                if has(f):
                    mixed(turn, f, 0)
                    mixed(turn, f, 1)
                if has(q):
                    take_oT()
                if has(b):
                    middle_part(qp[b % 2], q_rest, q_taken, q_mid, turn, b)
                    middle_part(kp[b % 2], k_rest, k_taken, k_mid, turn, b)
                if i == -2:
                    act.wait_ge(set_pe, 1)
                    nc.scalar.activation(tg[:], ps_s[0][:, 0:2], ACT.Tanh).then_inc(set_act, 1)

            steps(act, step)

        @block.vector
        def _(dve):
            def clear_vb(n):
                nc.vector.memset(vb[n][:], 0.0).then_inc(vb_cleared, 1)
                dve.wait_ge(vb_cleared, n + 1)
                for h2 in range(2):
                    nc.vector.memset(vb[n][64 * h2:64 * h2 + 64, :, :, 16 * h2 + DH:16 * h2 + DH + 1], 1.0).then_inc(vb_ones, 1)

            def order_qk():
                dve.wait_ge(w_qk_in, 16 * 4)
                nc.vector.tensor_copy(b_rowp[:].rearrange("p o (r a) -> p o r a", a=PAIRS),
                                      b_row[:].rearrange("p o (a r) -> p o r a", a=PAIRS)).then_inc(qk_cols, 1)
                for dst, src in ((wq_p, wq), (wk_p, wk)):
                    nc.vector.tensor_copy(dst[:].rearrange("p (r a) -> p r a", a=PAIRS), src[:].rearrange("p (a r) -> p r a", a=PAIRS)).then_inc(qk_cols, 1)
                dve.wait_ge(bias_filled, 1)
                nc.vector.tensor_copy(bias[:], bank[0][:, 0:2]).then_inc(bias_ready, 1)

            def set_up():
                dve.wait_ge(w_in, 16 * 9)
                nc.vector.tensor_copy(bv_rep[:], bv_col[:].to_broadcast([P, P])).then_inc(set_dve, 1)
                dve.wait_ge(set_pe, 2)
                nc.vector.tensor_copy(wrT[:], ps_s[1][:, 0:EXPERTS]).then_inc(set_dve, 1)
                dve.wait_ge(set_pe, 3)
                nc.vector.tensor_copy(bwT[:].rearrange("p e d -> p (e d)"), bank[2][:]).then_inc(set_dve, 1)
                dve.wait_ge(set_act, 1)
                nc.vector.tensor_scalar(wo_g[:], wo[:], tg[:, 0:1], None, ALU.mult).then_inc(set_dve, 1)

            def set_up_products():
                dve.wait_ge(set_pe, 4)
                nc.vector.tensor_scalar(c_rep[:], ps_s[0][:, 128:256], tg[:, 0:1], None, ALU.mult).then_inc(set_dve, 1)
                for n in range(2):
                    dve.wait_ge(set_pe, 5 + n)
                    nc.vector.tensor_scalar(mix_h[:, n:EXPERTS:2, :], bank[1 + n][:].rearrange("p (e d) -> p e d", d=D),
                                            tg[:, 1:2], None, ALU.mult).then_inc(set_dve, 1)

            def layer_norm(stats_sem, stats, mean_var, norm, src, turn, c):
                for t in range(TILES):
                    last = nc.vector.bn_stats(stats[:, t, :], src[:, t, :])
                last.then_inc(stats_sem, 1)
                wait_chunk(dve, stats_sem, 4, turn, c, 1)
                dve.sem_inc(dve_waited, 1)
                for t in range(TILES):
                    last = nc.vector.bn_aggr(mean_var[:, t, :], stats[:, t, :])
                last.then_inc(stats_sem, 1)
                wait_chunk(dve, stats_sem, 4, turn, c, 2)
                nc.vector.tensor_scalar(norm[:, 1, :], mean_var[:, :, 1], EPS, None, ALU.add).then_inc(stats_sem, 1)
                nc.vector.tensor_scalar(norm[:, 0, :], mean_var[:, :, 0], -1.0, None, ALU.mult).then_inc(stats_sem, 1)

            def rest_of(p, rest, src, col, high, taken, low, turn, b):
                wait_chunk(dve, high, 1, turn, b, 1)
                wait_chunk(dve, low, 1, turn, b - 1, 1)
                nc.vector.scalar_tensor_tensor(rest[:], src[:], bias[:, col:col + 1], p[:, 0, :],
                                               ALU.add, ALU.subtract).then_inc(taken, 1)

            def row_max(turn, i, fill):
                wait_chunk(dve, s_filled, PAIRS, turn, i, fill + 1)
                t, half = fill // 2, fill % 2
                nc.vector.tensor_reduce(nmax[:, :, 4 * half:4 * half + 4, t].rearrange("p g a -> p a g"),
                                        ps_s[fill % 2][:].rearrange("p (a g k) -> p a g k", g=2, k=SEQ),
                                        AX_X, ALU.max, negate=True).then_inc(s_max, 1)

            def normalise(turn, q, half):
                wait_chunk(dve, otr_filled, 2, turn, q, half + 1)
                blocks = back_bank(q, half)[:].rearrange("p (m w) -> p m w", w=16)
                nc.vector.reciprocal(rden[:, half, :], blocks[:, :, DH]).then_inc(rden_ready, 1)
                wait_chunk(dve, rden_ready, 2, turn, q, half + 1)
                wait_chunk(dve, oT_filled, 1, turn, q - 1, 1)
                nc.vector.tensor_tensor(o_tok[:, :, 64 * half:64 * half + 64].rearrange("p t (m d) -> p t m d", d=DH),
                                        blocks[:, :, 0:DH].rearrange("p (t m) d -> p t m d", t=TILES),
                                        rden[:, half, :].rearrange("p (t m o) -> p t m o", t=TILES, o=1).to_broadcast([P, TILES, 8, DH]),
                                        ALU.mult).then_inc(o_normed, 1)

            def top_two(turn, f):
                wait_chunk(dve, logit_filled, 1, turn, f, 1)
                nc.vector.tensor_copy(logit[:], bank[2][0:CB, 0:EXPERTS]).then_inc(gate_steps, 1)
                wait_chunk(dve, gate_steps, 8, turn, f, 1)
                dve.sem_inc(dve_waited, 1)
                nc.vector.max(top[:], logit[:]).then_inc(gate_steps, 1)
                wait_chunk(dve, gate_steps, 8, turn, f, 2)
                nc.vector.tensor_tensor(gw[:, 0:1], top[:, 1:2], top[:, 0:1], ALU.subtract).then_inc(gate_diff, 1)
                nc.vector.max_index(top_i[:], top[:], logit[:]).then_inc(gate_steps, 1)

            def gate_shares(turn, f):
                wait_chunk(dve, gate_steps, 8, turn, f, 3)
                nc.vector.tensor_copy(top_f[:], top_i[:]).then_inc(gate_steps, 1)
                wait_chunk(dve, gate_exp, 1, turn, f, 1)
                nc.vector.tensor_scalar(gw[:, 2:3], gw[:, 1:2], 1.0, None, ALU.add).then_inc(gate_steps, 1)
                wait_chunk(dve, gate_steps, 8, turn, f, 5)
                nc.vector.reciprocal(gw[:, 3:4], gw[:, 2:3]).then_inc(gate_steps, 1)
                wait_chunk(dve, gate_steps, 8, turn, f, 6)
                nc.vector.tensor_tensor(gw[:, 4:5], gw[:, 1:2], gw[:, 3:4], ALU.mult).then_inc(gate_steps, 1)

            def gate_rows(turn, f):
                wait_chunk(dve, gate_steps, 8, turn, f, 7)
                nc.vector.tensor_scalar(gate_a[:], col_of[:], top_f[:, 0:1], gw[:, 3:4], ALU.is_equal, ALU.mult)
                nc.vector.tensor_scalar(gate_b[:], col_of[:], top_f[:, 1:2], gw[:, 4:5], ALU.is_equal, ALU.mult).then_inc(gate_steps, 1)
                wait_chunk(dve, gate_steps, 8, turn, f, 8)
                wait_chunk(dve, grep_filled, 1, turn, f - 1, 1)
                nc.vector.tensor_tensor(gates[:], gate_a[:, None, :].to_broadcast([CB, 16, EXPERTS]),
                                        gate_b[:, None, :].to_broadcast([CB, 16, EXPERTS]), ALU.add).then_inc(gates_ready, 1)

            def step(turn, i):
                a, b, q, f = i + 3, i + 2, i - 1, i - 2

                def statistics():
                    wait_half(dve, x_in, 16, turn, a)
                    wait_chunk(dve, xn_ready, TILES, turn, a - 1, TILES)
                    layer_norm(ln1_steps, stats1, mean_var1, norm1, xt[a % 2], turn, a)

                def split_maxima():
                    wait_chunk(dve, s_max, PAIRS, turn, i, PAIRS)
                    wait_chunk(dve, shiftT_filled, 1, turn, i - 1, 1)
                    flat = nmax[:].rearrange("p g a t -> p g (a t)")
                    nc.vector.tensor_copy(shift[:, :, 0, :], flat).then_inc(shift_hi, 1)
                    wait_chunk(dve, shift_hi, 1, turn, i, 1)
                    nc.vector.tensor_tensor(shift[:, :, 1, :], flat, shift[:, :, 0, :], ALU.subtract).then_inc(shift_ready, 1)

                def own_gates():
                    if f == 0:
                        dve.wait_ge(consts, 12)
                    wait_chunk(dve, grep_filled, 1, turn, f, 1)
                    wait_chunk(dve, wmix_filled, 2, turn, f - 1, 2)
                    nc.vector.tensor_tensor(gmix[:], bank[2][:, 0:CB].rearrange("p (b o) -> p b o", o=1).to_broadcast([P, CB, 16]),
                                            h16_mask[:, None, :].to_broadcast([P, CB, 16]), ALU.mult).then_inc(gmix_ready, 1)

                def q_low_rest():
                    rest_of(qp[b % 2], q_rest, ps_t[0], 0, q_high, q_taken, q_parts, turn, b)

                def k_low_rest():
                    rest_of(kp[b % 2], k_rest, ps_t[1], 1, k_high, k_taken, k_parts, turn, b)

                def result():
                    wait_chunk(dve, y2_filled, 1, turn, f, 1)
                    wait_chunk(dve, x1_scaled, TILES, turn, f, TILES)
                    flat = x1[f % 2][:].rearrange("p t d -> p (t d)")
                    nc.vector.tensor_tensor(flat, bank[2][:], flat, ALU.add).then_inc(out_ready, 1)

                def residual():
                    wait_chunk(dve, y_filled, 1, turn, q, 1)
                    wait_chunk(dve, xr_ready, 1, turn, q, 1)
                    wait_half(dve, out_done, 16, turn, q - 2)
                    nc.vector.tensor_tensor(x1[q % 2][:].rearrange("p t d -> p (t d)"), bank[1][:],
                                            xr[q % 2][:].rearrange("p t d -> p (t d)"), ALU.add).then_inc(x1_ready, 1)

                def x1_statistics():
                    wait_chunk(dve, x1_ready, 1, turn, q, 1)
                    wait_chunk(dve, x1_scaled, TILES, turn, q - 1, TILES)
                    layer_norm(ln2_steps, stats2, mean_var2, norm2, x1[q % 2], turn, q)

                if i == -3:
                    clear_vb(0)
                    statistics()
                    order_qk()
                    clear_vb(1)
                    return
                if i == -2:
                    statistics()
                    q_low_rest()
                    k_low_rest()
                    set_up()
                    return
                if i == -1:
                    q_low_rest()
                    k_low_rest()
                    set_up_products()
                    statistics()
                    return
                if i == CHUNKS:
                    top_two(turn, f)
                    normalise(turn, q, 0)
                    normalise(turn, q, 1)
                    gate_shares(turn, f)
                    gate_rows(turn, f)
                    residual()
                    own_gates()
                    x1_statistics()
                    result()
                    return
                if has(i):
                    for fill in range(6):
                        row_max(turn, i, fill)
                if has(f):
                    top_two(turn, f)
                    gate_shares(turn, f)
                if has(i):
                    row_max(turn, i, 6)
                if has(f):
                    gate_rows(turn, f)
                if has(i):
                    row_max(turn, i, 7)
                    split_maxima()
                if has(f):
                    own_gates()
                if has(q):
                    normalise(turn, q, 0)
                if has(b):
                    q_low_rest()
                if has(q):
                    normalise(turn, q, 1)
                if has(b):
                    k_low_rest()
                if has(a):
                    statistics()
                if has(f):
                    result()
                if has(q):
                    residual()
                    x1_statistics()

            steps(dve, step)

        @block.tensor
        def _(pe):
            mm = nc.tensor.matmul

            def tiles_T(dst, src):
                for t in range(TILES):
                    last = nc.tensor.transpose(dst[:, P * t:P * t + P], src[:, t, :], ident[:])
                return last

            pe.wait_ge(consts, 12)
            pe.wait_ge(qk_cols, 1)
            for n in range(2):
                last = mm(bank[0][:, n:n + 1], b_rowp[:, n, :], ones_f[:, 0:1], start=True, stop=True)
            last.then_inc(bias_filled, 1)

            def set_up():
                pe.wait_ge(w_in, 16 * 9)
                mm(ps_s[0][:, 0:2], ones_f[:], g_row[:], start=True, stop=True).then_inc(set_pe, 1)
                nc.tensor.transpose(ps_s[1][:, 0:EXPERTS], wr_in[:], ident[0:EXPERTS, 0:EXPERTS]).then_inc(set_pe, 1)
                for e4 in range(EXPERTS // 2):
                    last = nc.tensor.transpose(bank[2][:, D * e4:D * e4 + D], bw_in[:, e4, :], ident[:])
                last.then_inc(set_pe, 1)

            def set_up_products():
                pe.wait_ge(set_dve, 3)
                pe.wait_ge(set_act, 1)
                mm(ps_s[0][:, 128:256], bv_rep[:], wo[:], start=True, stop=False)
                mm(ps_s[0][:, 128:256], ones_f[:], bo_row[:], start=False, stop=True).then_inc(set_pe, 1)
                for e in range(EXPERTS):
                    e4, rows = e // 2, slice(RANK * (e % 2), RANK * (e % 2) + RANK)
                    last = mm(bank[1 + e % 2][:, D * e4:D * e4 + D], bwT[rows, e4, :], a_in[rows, e4, :], start=True, stop=True)
                    if e4 == 3:
                        last.then_inc(set_pe, 1)

            def key_scores(turn, q, pair):
                if pair == 0:
                    wait_half(pe, shift_in, 16, turn, q)
                    if q < 2:
                        pe.wait_ge(kb_ones[q], 32)
                if pair >= 2:
                    wait_chunk(pe, t_exp, PAIRS, turn, q, pair - 1)
                elif q < CHUNKS - 2:
                    wait_chunk(pe, (q_taken, k_taken)[pair], 1, turn, q + 2, 1)
                else:
                    wait_chunk(pe, t_exp, PAIRS, turn, q - 1, PAIRS - 1 + pair)
                n = q % 2
                for b in range(CB):
                    cols = slice(SEQ * b, SEQ * b + SEQ)
                    last = mm(ps_t[pair % 2][:, cols], kb[n][0:ROWS + SHIFT, pair, b, :, :], qa[n][0:ROWS + SHIFT, pair, cols],
                              start=True, stop=True)
                last.then_inc(t_filled, 1)

            def query_scores(turn, i, fill):
                if fill == 0:
                    wait_half(pe, qa_in, 16 * TERMS, turn, i)
                    wait_half(pe, kb_in, 32 * TERMS, turn, i)
                if fill == 0 and i >= 2:
                    wait_chunk(pe, oT_taken, 1, turn, i - 2, 1)
                elif fill == 1 and i >= 3:
                    wait_chunk(pe, wmix_taken, 2, turn, i - 3, 2)
                else:
                    wait_chunk(pe, s_max, PAIRS, turn, i - (fill < 2), (fill - 2) % PAIRS + 1)
                n, t = i % 2, fill // 2
                for a in range(4):
                    pair = 4 * (fill % 2) + a
                    for b2 in range(2):
                        cols = slice(P * t + SEQ * b2, P * t + SEQ * b2 + SEQ)
                        last = mm(ps_s[fill % 2][SEQ * b2:SEQ * b2 + SEQ, P * a:P * a + P], qa[n][0:ROWS, pair, cols],
                                  kb[n][0:ROWS, pair, 2 * t + b2, :, :], start=True, stop=True)
                last.then_inc(s_filled, 1)

            def times_v(turn, q, half, batches):
                if batches[0] == 0:
                    wait_chunk(pe, t_exp, PAIRS, turn, q, 4 * half + 4)
                    wait_chunk(pe, o_taken, 2, turn, q - (half == 0), 2 - half)
                    if half == 0:
                        wait_chunk(pe, v_taken, 2, turn, q, 2)
                for b in batches:
                    cols = slice(SEQ * b, SEQ * b + SEQ)
                    for a in range(4):
                        last = mm(ps_o[VW * a:VW * a + VW, cols], vb[q % 2][:, b, 4 * half + a, :], prob[:, 4 * half + a, cols],
                                  start=True, stop=True, tile_position=(0, VW * a))
                return last

            def o_back(turn, q, half):
                wait_chunk(pe, o_taken, 2, turn, q, half + 1)
                if half == 0:
                    wait_chunk(pe, x1_ready, 1, turn, q - 1, 1)
                elif q < CHUNKS - 1:
                    wait_chunk(pe, shiftT_taken, 1, turn, q + 1, 1)
                else:
                    wait_chunk(pe, t_exp, PAIRS, turn, q, PAIRS - 1)
                for t in range(TILES):
                    last = nc.tensor.transpose(back_bank(q, half)[:, P * t:P * t + P], oaug[:, half, P * t:P * t + P], ident[:])
                last.then_inc(otr_filled, 1)

            def mix_half(turn, f, n):
                if f == 0:
                    pe.wait_ge(mix_in, 16 * HC)
                wait_chunk(pe, gmix_ready, 1, turn, f, 1)
                if f == CHUNKS - 2 and n == 0:
                    wait_chunk(pe, oT_taken, 1, turn, f + 1, 1)
                elif f < CHUNKS - 2:
                    wait_chunk(pe, s_max, PAIRS, turn, f + 2, PAIRS - 1 + n)
                else:
                    wait_chunk(pe, wmix_taken, 2, turn, f - 1, n + 1)
                for hc in range(4):
                    last = mm(ps_s[n][:, P * hc:P * hc + P], mix[:, 4 * n + hc, :], gmix[:].rearrange("p b h -> p (b h)"),
                              start=True, stop=True)
                last.then_inc(wmix_filled, 1)

            def step(turn, i):
                b, v, q, f = i + 2, i + 1, i - 1, i - 2

                def values(c, batches):
                    for bb in batches:
                        for h2 in range(2):
                            last = mm(bank[0][64 * h2:64 * h2 + 64, 64 * bb:64 * bb + 64], cT[c % 2][:, SEQ * bb:SEQ * bb + SEQ],
                                      wv[:].rearrange("p (a g d) -> p g a d", g=2, d=DH)[:, h2], start=True, stop=True)
                    return last

                def shift_rows():
                    wait_chunk(pe, shift_ready, 1, turn, i, 1)
                    if has(f):
                        wait_chunk(pe, gmix_ready, 1, turn, f, 1)
                    elif i == 0:
                        pe.wait_ge(set_dve, 7)
                    else:
                        wait_chunk(pe, shiftT_taken, 1, turn, i - 1, 1)
                    nc.tensor.transpose(bank[2][:, 0:64].bitcast(BF16), shift[:].rearrange("p g h m -> p (g h m)"), identb[:]).then_inc(shiftT_filled, 1)

                def inputs_T():
                    wait_chunk(pe, xn_ready, TILES, turn, b, TILES)
                    if b >= 3:
                        wait_chunk(pe, t_exp, PAIRS, turn, b - 3, PAIRS - 1)
                    else:
                        wait_chunk(pe, q_taken, 1, turn, b - 1, 1)
                    tiles_T(ps_t[0], xn).then_inc(xnT_filled, 1)
                    wait_half(pe, c_in, 16, turn, b)
                    if b >= 3:
                        wait_chunk(pe, t_exp, PAIRS, turn, b - 3, PAIRS)
                    else:
                        wait_chunk(pe, k_taken, 1, turn, b - 1, 1)
                    tiles_T(ps_t[1], ct[b % 2]).then_inc(cT_filled, 1)

                def q_projection():
                    if b == 0:
                        pe.wait_ge(qk_cols, 3)
                    wait_chunk(pe, xnT_taken, 1, turn, b, 1)
                    mm(ps_t[0][:], wq_p[:], xnT[:], start=True, stop=True).then_inc(q_filled, 1)

                def k_projection():
                    wait_chunk(pe, cT_taken, 1, turn, b, 1)
                    mm(ps_t[1][:], wk_p[:], cT[b % 2][:], start=True, stop=True).then_inc(k_filled, 1)

                def first_values():
                    if b == 0:
                        pe.wait_ge(bias_ready, 1)
                        pe.wait_ge(w_in, 16 * 9)
                    wait_chunk(pe, v_taken, 2, turn, b - 1, 2)
                    values(b, range(CB // 2))

                def x2_T():
                    wait_chunk(pe, xn2_ready, TILES, turn, f, TILES)
                    if f >= 1:
                        wait_chunk(pe, out_ready, 1, turn, f - 1, 1)
                    else:
                        wait_chunk(pe, o_normed, 2, turn, f, 2)
                    tiles_T(bank[2], xn2).then_inc(x2T_filled, 1)

                def router():
                    wait_chunk(pe, x2T_taken, 1, turn, f, 1)
                    mm(bank[2][0:CB, 0:EXPERTS], x2T[:, 0:TOK:SEQ], wrT[:], start=True, stop=True).then_inc(logit_filled, 1)

                def spread_gates():
                    wait_chunk(pe, gates_ready, 1, turn, f, 1)
                    mm(bank[2][:, 0:CB], gates[:].rearrange("b h e -> b (h e)"), ident[0:CB, 0:CB],
                       start=True, stop=True).then_inc(grep_filled, 1)

                def heads_T():
                    wait_chunk(pe, o_normed, 2, turn, q, 2)
                    if i == CHUNKS:
                        wait_chunk(pe, wmix_taken, 2, turn, f - 1, 1)
                    elif has(f):
                        wait_chunk(pe, wmix_taken, 2, turn, f, 1)
                    else:
                        wait_chunk(pe, s_max, PAIRS, turn, i, PAIRS - 1)
                    tiles_T(ps_s[0], o_tok).then_inc(oT_filled, 1)

                def attention_out():
                    wait_chunk(pe, oT_taken, 1, turn, q, 1)
                    for t in range(TILES):
                        last = mm(bank[1][:, D * t:D * t + D], oT[:, P * t:P * t + P], wo_g[:], start=True, stop=True)
                    last.then_inc(y_filled, 1)

                def experts_out():
                    wait_chunk(pe, wmix_taken, 2, turn, f, 2)
                    if f < CHUNKS - 1:
                        wait_chunk(pe, o_normed, 2, turn, f + 1, 2)
                    for bb in range(CB):
                        rows = slice(64 * (bb % 2), 64 * (bb % 2) + 64)
                        last = mm(bank[2][rows, D * (bb // 2):D * (bb // 2) + D], x2T[:, SEQ * bb:SEQ * bb + SEQ], wmix[:, bb, :],
                                  start=True, stop=True)
                    last.then_inc(y2_filled, 1)

                if i == 0:
                    values(v, range(CB // 2, CB)).then_inc(v_filled, 1)
                    pe.wait_ge(set_dve, 5)
                    for fill in range(PAIRS):
                        query_scores(turn, i, fill)
                    inputs_T()
                    shift_rows()
                    q_projection()
                    k_projection()
                    first_values()
                    return
                if i == CHUNKS:
                    for pair in range(6):
                        key_scores(turn, q, pair)
                    times_v(turn, q, 0, range(CB // 2))
                    key_scores(turn, q, 6)
                    times_v(turn, q, 0, range(CB // 2, CB)).then_inc(o_filled, 1)
                    key_scores(turn, q, 7)
                    x2_T()
                    times_v(turn, q, 1, range(CB // 2))
                    router()
                    times_v(turn, q, 1, range(CB // 2, CB)).then_inc(o_filled, 1)
                    o_back(turn, q, 0)
                    o_back(turn, q, 1)
                    heads_T()
                    attention_out()
                    spread_gates()
                    mix_half(turn, f, 0)
                    mix_half(turn, f, 1)
                    experts_out()
                    return
                if has(q):
                    key_scores(turn, q, 0)
                    key_scores(turn, q, 1)
                if has(v):
                    values(v, range(CB // 2, CB)).then_inc(v_filled, 1)
                if has(q):
                    key_scores(turn, q, 2)
                    key_scores(turn, q, 3)
                if has(i):
                    query_scores(turn, i, 0)
                    query_scores(turn, i, 1)
                if has(q):
                    key_scores(turn, q, 4)
                    key_scores(turn, q, 5)
                    times_v(turn, q, 0, range(CB // 2))
                    key_scores(turn, q, 6)
                if has(i):
                    query_scores(turn, i, 2)
                if has(q):
                    key_scores(turn, q, 7)
                if has(i):
                    query_scores(turn, i, 3)
                if has(q):
                    times_v(turn, q, 0, range(CB // 2, CB)).then_inc(o_filled, 1)
                if has(i):
                    query_scores(turn, i, 4)
                    query_scores(turn, i, 5)
                if has(f):
                    x2_T()
                if has(q):
                    times_v(turn, q, 1, range(CB // 2))
                if has(f):
                    router()
                if has(q):
                    times_v(turn, q, 1, range(CB // 2, CB)).then_inc(o_filled, 1)
                if has(i):
                    query_scores(turn, i, 6)
                if has(b):
                    inputs_T()
                if has(i):
                    query_scores(turn, i, 7)
                if has(q):
                    o_back(turn, q, 0)
                if has(b):
                    q_projection()
                if has(f):
                    spread_gates()
                if has(b):
                    k_projection()
                if has(i):
                    shift_rows()
                if has(f):
                    mix_half(turn, f, 0)
                if has(q):
                    o_back(turn, q, 1)
                if has(f):
                    mix_half(turn, f, 1)
                if has(b):
                    first_values()
                if has(q):
                    heads_T()
                if has(f):
                    experts_out()
                if has(q):
                    attention_out()
                if i == -2:
                    set_up()
                if i == -1:
                    set_up_products()

            steps(pe, step)


_INS = ['x', 'ctx_1024', 'g_xattn', 'g_ffn', 'L0_xattn_Wq', 'L0_xattn_bq', 'L0_xattn_Wk', 'L0_xattn_bk', 'L0_xattn_Wv',
        'L0_xattn_bv', 'L0_xattn_Wo', 'L0_xattn_bo', 'L0_ffn_Wr', 'L0_ffn_A', 'L0_ffn_Bw']


def kernel(**inputs):
    import numpy as _np
    import concourse.bacc as _bacc
    from concourse import mybir as _mybir
    from concourse.bass_utils import run_bass_kernel_spmd as _run

    nc = _bacc.Bacc("TRN2", target_bir_lowering=False, num_devices=1)
    arrays, args = {}, []
    for name in _INS:
        a = _np.ascontiguousarray(inputs[name])
        arrays[f"in_{name}_dram"] = a
        args.append(nc.dram_tensor(f"in_{name}_dram", a.shape, _mybir.dt.from_np(a.dtype), kind="ExternalInput").ap())
    args.append(nc.dram_tensor("out_0_dram", (BATCHES, SEQ, D), _mybir.dt.float32, kind="ExternalOutput").ap())
    block_attention_experts(nc, *args)
    r = _run(nc, [arrays], core_ids=[0])
    return r.results[0]["out_0_dram"]
```
